# Optimizing a Trainium2 kernel written in Bass

```python
import numpy as np
import jax
import jax.numpy as jnp

def _softmax(x, axis=-1):
    return jax.nn.softmax(x, axis=axis)

def _gelu(x):
    return jax.nn.gelu(x, approximate=True)

def _silu(x):
    return jax.nn.silu(x)

def _sigmoid(x):
    return jax.nn.sigmoid(x)

def _layernorm(x, axis=-1, eps=1e-05):
    m = jnp.mean(x, axis=axis, keepdims=True)
    v = jnp.var(x, axis=axis, keepdims=True)
    return (x - m) / jnp.sqrt(v + eps)

def _scatter_add(tgt, idx, src, axis=0):
    return tgt.at[idx].add(src)

def _segment_sum(src, seg, n):
    return jax.ops.segment_sum(src, seg, n)
kernel_name = 'mk_seq_preln_d1_jaxref_r4_bd7513'

def setup_inputs(seed: int=0):
    np.random.seed(seed)
    _w = jnp.asarray

    def _L0_attn_setup():
        import jax, jax.numpy as jnp
        import numpy as np
        D_MODEL = 256
        N_HEADS = 16
        DH = D_MODEL // N_HEADS
        B, T = (4, 512)
        ROPE_BASE = 10000.0
        EPS = 1e-06

        def _rope(q, k, base=ROPE_BASE):
            half = q.shape[-1] // 2
            freqs = jnp.arange(half, dtype=q.dtype)
            inv_freq = base ** (-freqs / half)
            pos = jnp.arange(q.shape[2], dtype=q.dtype)
            ang = pos[:, None] * inv_freq[None, :]
            c = jnp.cos(ang)[None, None]
            s = jnp.sin(ang)[None, None]

            def rot(x):
                x1 = x[..., :half]
                x2 = x[..., half:2 * half]
                return jnp.concatenate([x1 * c - x2 * s, x1 * s + x2 * c], axis=-1)
            return (rot(q), rot(k))

        def _phi(x):
            return jax.nn.elu(x) + 1.0

        def _forward(x, Wq, Wk, Wv, Wo):
            Bx, Tx, D = x.shape
            H, dh = (N_HEADS, D // N_HEADS)
            q = (x @ Wq.T).reshape(Bx, Tx, H, dh).transpose(0, 2, 1, 3)
            k = (x @ Wk.T).reshape(Bx, Tx, H, dh).transpose(0, 2, 1, 3)
            v = (x @ Wv.T).reshape(Bx, Tx, H, dh).transpose(0, 2, 1, 3)
            q, k = _rope(q, k)
            q = _phi(q)
            k = _phi(k)
            qT = q.transpose(2, 0, 1, 3)
            kT = k.transpose(2, 0, 1, 3)
            vT = v.transpose(2, 0, 1, 3)

            def step(carry, qkv):
                K_sum, KV = carry
                q_t, k_t, v_t = qkv
                K_sum = K_sum + k_t
                KV = KV + k_t[..., :, None] * v_t[..., None, :]
                num = jnp.einsum('bhd,bhde->bhe', q_t, KV)
                den = jnp.maximum(jnp.einsum('bhd,bhd->bh', q_t, K_sum), EPS)
                return ((K_sum, KV), num / den[..., None])
            init = (jnp.zeros((Bx, H, dh), x.dtype), jnp.zeros((Bx, H, dh, dh), x.dtype))
            _, Y = jax.lax.scan(step, init, (qT, kT, vT))
            Y = Y.transpose(1, 0, 2, 3).reshape(Bx, Tx, D)
            return Y @ Wo.T
        key = jax.random.key(seed)
        kx, kq, kk, kv, ko = jax.random.split(key, 5)
        scale = 0.02
        return {'x': jax.random.normal(kx, (B, T, D_MODEL), jnp.float32), 'Wq': jax.random.normal(kq, (D_MODEL, D_MODEL), jnp.float32) * scale, 'Wk': jax.random.normal(kk, (D_MODEL, D_MODEL), jnp.float32) * scale, 'Wv': jax.random.normal(kv, (D_MODEL, D_MODEL), jnp.float32) * scale, 'Wo': jax.random.normal(ko, (D_MODEL, D_MODEL), jnp.float32) * scale}
    _L0_attn_in = _L0_attn_setup()

    def _L0_ffn_setup():
        import jax, jax.numpy as jnp
        import numpy as np
        DIM = 256
        HIDDEN = 512
        N_EXPERTS = 8
        TOP_K = 2
        EPS = 1e-06

        def rms_norm(x, scale, eps=EPS):
            ms = jnp.mean(jnp.square(x.astype(jnp.float32)), axis=-1, keepdims=True)
            s = scale.astype(jnp.float32) * jax.lax.rsqrt(ms + eps)
            return x * s.astype(x.dtype)

        def moe_linear(xf, ids, W):
            E = W.shape[0]
            out = jnp.zeros((xf.shape[0], W.shape[1]), dtype=xf.dtype)
            for e in range(E):
                out = out + jnp.where((ids == e)[:, None], xf @ W[e].T, 0.0)
            return out
        key = jax.random.key(seed)
        k1, k2, k3, k4 = jax.random.split(key, 4)
        x = jax.random.normal(k1, (4, 1024, DIM), dtype=jnp.float32)
        norm_scale = jnp.ones((DIM,), dtype=jnp.float32)
        w_router = jax.random.normal(k2, (N_EXPERTS, DIM), dtype=jnp.float32) / np.sqrt(DIM)
        lim_up = np.sqrt(6.0 / (DIM + 2 * HIDDEN))
        w_up = jax.random.uniform(k3, (N_EXPERTS, 2 * HIDDEN, DIM), dtype=jnp.float32, minval=-lim_up, maxval=lim_up)
        lim_dn = np.sqrt(6.0 / (HIDDEN + DIM))
        w_down = jax.random.uniform(k4, (N_EXPERTS, DIM, HIDDEN), dtype=jnp.float32, minval=-lim_dn, maxval=lim_dn)
        return {'x': x, 'norm_scale': norm_scale, 'w_router': w_router, 'w_up': w_up, 'w_down': w_down}
    _L0_ffn_in = _L0_ffn_setup()
    _d = {'L0_attn_x': _L0_attn_in['x'], 'L0_attn_Wq': _L0_attn_in['Wq'], 'L0_attn_Wk': _L0_attn_in['Wk'], 'L0_attn_Wv': _L0_attn_in['Wv'], 'L0_attn_Wo': _L0_attn_in['Wo'], 'L0_ffn_norm_scale': _L0_ffn_in['norm_scale'], 'L0_ffn_w_router': _L0_ffn_in['w_router'], 'L0_ffn_w_up': _L0_ffn_in['w_up'], 'L0_ffn_w_down': _L0_ffn_in['w_down']}
    _x0 = _d['L0_attn_x']
    _d['L0_attn_x'] = jax.random.normal(jax.random.fold_in(jax.random.key(seed), 1), (2, 2048, 256), dtype=_x0.dtype)
    del _x0
    return _d

def reference(L0_attn_x, L0_attn_Wq, L0_attn_Wk, L0_attn_Wv, L0_attn_Wo, L0_ffn_norm_scale, L0_ffn_w_router, L0_ffn_w_up, L0_ffn_w_down):

    def _L0_attn_ref(x, Wq, Wk, Wv, Wo):
        import jax, jax.numpy as jnp
        import numpy as np
        D_MODEL = 256
        N_HEADS = 16
        DH = D_MODEL // N_HEADS
        B, T = (4, 512)
        ROPE_BASE = 10000.0
        EPS = 1e-06

        def _rope(q, k, base=ROPE_BASE):
            half = q.shape[-1] // 2
            freqs = jnp.arange(half, dtype=q.dtype)
            inv_freq = base ** (-freqs / half)
            pos = jnp.arange(q.shape[2], dtype=q.dtype)
            ang = pos[:, None] * inv_freq[None, :]
            c = jnp.cos(ang)[None, None]
            s = jnp.sin(ang)[None, None]

            def rot(x):
                x1 = x[..., :half]
                x2 = x[..., half:2 * half]
                return jnp.concatenate([x1 * c - x2 * s, x1 * s + x2 * c], axis=-1)
            return (rot(q), rot(k))

        def _phi(x):
            return jax.nn.elu(x) + 1.0

        def _forward(x, Wq, Wk, Wv, Wo):
            Bx, Tx, D = x.shape
            H, dh = (N_HEADS, D // N_HEADS)
            q = (x @ Wq.T).reshape(Bx, Tx, H, dh).transpose(0, 2, 1, 3)
            k = (x @ Wk.T).reshape(Bx, Tx, H, dh).transpose(0, 2, 1, 3)
            v = (x @ Wv.T).reshape(Bx, Tx, H, dh).transpose(0, 2, 1, 3)
            q, k = _rope(q, k)
            q = _phi(q)
            k = _phi(k)
            qT = q.transpose(2, 0, 1, 3)
            kT = k.transpose(2, 0, 1, 3)
            vT = v.transpose(2, 0, 1, 3)

            def step(carry, qkv):
                K_sum, KV = carry
                q_t, k_t, v_t = qkv
                K_sum = K_sum + k_t
                KV = KV + k_t[..., :, None] * v_t[..., None, :]
                num = jnp.einsum('bhd,bhde->bhe', q_t, KV)
                den = jnp.maximum(jnp.einsum('bhd,bhd->bh', q_t, K_sum), EPS)
                return ((K_sum, KV), num / den[..., None])
            init = (jnp.zeros((Bx, H, dh), x.dtype), jnp.zeros((Bx, H, dh, dh), x.dtype))
            _, Y = jax.lax.scan(step, init, (qT, kT, vT))
            Y = Y.transpose(1, 0, 2, 3).reshape(Bx, Tx, D)
            return Y @ Wo.T
        return _forward(x, Wq, Wk, Wv, Wo)

    def _L0_ffn_ref(x, norm_scale, w_router, w_up, w_down):
        import jax, jax.numpy as jnp
        import numpy as np
        DIM = 256
        HIDDEN = 512
        N_EXPERTS = 8
        TOP_K = 2
        EPS = 1e-06

        def rms_norm(x, scale, eps=EPS):
            ms = jnp.mean(jnp.square(x.astype(jnp.float32)), axis=-1, keepdims=True)
            s = scale.astype(jnp.float32) * jax.lax.rsqrt(ms + eps)
            return x * s.astype(x.dtype)

        def moe_linear(xf, ids, W):
            E = W.shape[0]
            out = jnp.zeros((xf.shape[0], W.shape[1]), dtype=xf.dtype)
            for e in range(E):
                out = out + jnp.where((ids == e)[:, None], xf @ W[e].T, 0.0)
            return out
        B, S, D = x.shape
        skip = x
        xn = rms_norm(x, norm_scale)
        scores = (xn @ w_router.T).astype(jnp.float32)
        scores_topk, idx = jax.lax.top_k(scores, TOP_K)
        weights = jax.nn.softmax(scores_topk, axis=-1)
        xf = jnp.broadcast_to(xn[..., None, :], (B, S, TOP_K, D)).reshape(-1, D)
        ids = idx.reshape(-1)
        up = moe_linear(xf, ids, w_up)
        u, gate = jnp.split(up, 2, axis=-1)
        h = u * jax.nn.silu(gate)
        down = moe_linear(h, ids, w_down)
        down = down.reshape(B, S, TOP_K, D)
        out = jnp.sum(down * weights[..., None].astype(down.dtype), axis=-2)
        return out + skip
    x = L0_attn_x
    x = x + _L0_attn_ref(_layernorm(x, axis=-1), L0_attn_Wq, L0_attn_Wk, L0_attn_Wv, L0_attn_Wo)
    x = x + _L0_ffn_ref(_layernorm(x, axis=-1), L0_ffn_norm_scale, L0_ffn_w_router, L0_ffn_w_up, L0_ffn_w_down)
    return x

_drawn_inputs = setup_inputs


def setup_inputs(seed=0):
    import zlib

    import numpy as np

    out = dict(_drawn_inputs(seed))
    spreads = {'L0_ffn_norm_scale': (1.0, 0.2)}
    factors = {'L0_attn_Wq': 8.0, 'L0_attn_Wk': 8.0, 'L0_attn_Wv': 7.105, 'L0_attn_Wo': 7.157}
    for name, (base, spread) in spreads.items():
        noise = np.random.default_rng([zlib.crc32(name.encode()), seed]).standard_normal(out[name].shape)
        drawn = base * np.exp(spread * noise) if base else spread * noise
        out[name] = jnp.asarray(drawn.astype(out[name].dtype))
    for name, factor in factors.items():
        out[name] = (out[name] * factor).astype(out[name].dtype)
    return out
```

```python
from contextlib import ExitStack

import concourse.bass as bass
from concourse import mybir

P = 128
ALU = mybir.AluOpType
ACT = mybir.ActivationFunctionType
F32 = mybir.dt.float32
BF16 = mybir.dt.bfloat16
U32 = mybir.dt.uint32
AX_X = mybir.AxisListType.X

LN_EPS, RMS_EPS, DEN_EPS = 1e-5, 1e-6, 1e-6
HEAD_DIM = 16
ROW = 260
TOKEN, W_SECOND, W_GAP, FIRST_EXPERT = 256, 257, 258, 259
RING = 4


def sizes(batches, length, dim, experts, hidden):
    tokens = batches * length
    tiles = tokens // P
    region = tokens + P
    routed = (2 * tokens + experts * (P - 1)) // P
    return tokens, tiles, region, routed


class Steps:

    def __init__(self, eng, sem, n, per_tile):
        self.eng, self.sem, self.base, self.per_tile, self.count = eng, sem, n * per_tile, per_tile, 0

    def done(self, ins):
        self.count += 1
        ins.then_inc(self.sem, 1)
        self.eng.wait_ge(self.sem, self.base + self.count)

    def close(self):
        assert self.count == self.per_tile, self.count


def block_kernel(nc, x, w_qk, w_v, w_o, rope, norm_scale, w_router, w_up, w_down, consts_f, consts_b,
                 token_ids, routed_rows, out, batches, length, experts, hidden):
    dim = x.shape[1]
    tokens, tiles, region, routed_tiles = sizes(batches, length, dim, experts, hidden)
    per_batch = tiles // batches
    heads = dim // HEAD_DIM
    KC = dim // P
    HC = hidden // P
    pad_region = experts * region
    assert batches == 2 and KC == 2 and heads == 16 and tiles % RING == 0 and HC == 4
    assert experts == 8 and hidden == 512

    x_out = out[0:tokens, :]

    with ExitStack() as ctx:
        def sb(name, shape, dt=F32):
            return ctx.enter_context(nc.sbuf_tensor(name, shape, dt))

        def psum(name, shape):
            return ctx.enter_context(nc.psum_tensor(name, shape, F32))

        def sem(name):
            return ctx.enter_context(nc.semaphore(name))

        wqk_sb = sb("wqk_sb", [P, KC, 2 * dim])
        wv_sb = sb("wv_sb", [P, KC, dim])
        wo_sb = sb("wo_sb", [P, KC, dim])
        wr_sb = sb("wr_sb", [P, KC, experts])
        rope_sb = sb("rope_sb", [P, per_batch, 2 * HEAD_DIM])
        scale_sb = sb("scale_sb", [P, dim])
        up_sb = sb("up_sb", [P, experts, KC * 2 * hidden])
        down_sb = sb("down_sb", [P, experts, HC * dim])
        NF = consts_f.shape[1]
        cf = sb("cf", [P, NF])
        ident = cf[:, 0:P]
        causal = cf[:, P:2 * P]
        ones = cf[:, 2 * P:3 * P]
        same_head = cf[:, 3 * P:4 * P]
        at = 4 * P
        parity_mask = cf[:, at:at + 2]
        at += 2
        expert_iota = cf[:, at:at + experts]
        at += experts
        tile_starts = cf[:, at:at + 32]
        at += 32
        low_tri = cf[:, at:at + experts * experts]
        at += experts * experts
        tile_iota = cf[:, at:at + routed_tiles]
        at += routed_tiles
        region_start = cf[:, at:at + experts]
        at += experts
        minus_half = cf[:, at:at + 1]
        at += 1
        assert at == NF
        cb = sb("cb", [P, 2 * P], BF16)
        earlier = cb[:, 0:P]
        ones_b = cb[:, P:2 * P]
        ids = sb("ids", [P, tiles + 1], U32)

        xin = sb("xin", [P, RING, dim])
        stats1 = sb("stats1", [P, 2, 6])
        mv1 = sb("mv1", [P, 2, 2])
        rstd1 = sb("rstd1", [P, 2, 1])
        xhat = sb("xhat", [P, 2, dim])
        xhatT = sb("xhatT", [P, 2, KC, P])
        rot_a = sb("rot_a", [P, 2 * dim])
        rot_b = sb("rot_b", [P, 2 * dim])
        rot = sb("rot", [P, 2 * dim])
        erot = sb("erot", [P, 2 * dim])
        emin = sb("emin", [P, 2 * dim])
        phi = sb("phi", [P, 2, 2 * dim])
        v_pad = sb("v_pad", [P, 2, heads, 2 * HEAD_DIM])
        kacc = sb("kacc", [P, 2, dim])
        qk_prod = sb("qk_prod", [P, dim])
        den = sb("den", [P, heads])
        rden = sb("rden", [P, heads])
        qn = sb("qn", [P, dim])
        kT = sb("kT", [P, KC, P])
        qT = sb("qT", [P, KC, P])
        q_par = sb("q_par", [P, KC, 2, P])
        attn = sb("attn", [P, 4, KC, 2, P])
        state = sb("state", [P, 2, KC, P])
        state_add = sb("state_add", [P, KC, P])
        yT = sb("yT", [P, KC, P])
        x1 = sb("x1", [P, dim])
        stats2 = sb("stats2", [P, 6])
        mv2 = sb("mv2", [P, 2])
        rstd2 = sb("rstd2", [P, 1])
        ms2 = sb("ms2", [P, 1])
        var1 = sb("var1", [P, 1])
        var2 = sb("var2", [P, 1])
        rms2 = sb("rms2", [P, 1])
        xhat2 = sb("xhat2", [P, dim])
        acc = sb("acc", [P, RING, dim])
        rows = sb("rows", [P, RING, ROW])
        xnT = sb("xnT", [P, KC, P])
        scores8 = sb("scores8", [P, experts])
        top8 = sb("top8", [P, 8])
        top8_at = sb("top8_at", [P, 8], U32)
        chosen = sb("chosen", [P, 2, 2])
        onehot = sb("onehot", [P, 2, 2, experts])
        gap = sb("gap", [P, 1])
        egap = sb("egap", [P, 1])
        gap1 = sb("gap1", [P, 1])
        w_first = sb("w_first", [P, 1])
        members = sb("members", [P, 2, experts], BF16)
        macc = sb("macc", [P, experts], BF16)
        rank_prod = sb("rank_prod", [P, 2, experts])
        rank = sb("rank", [P, 2])
        slot_of = sb("slot_of", [P, 2, 2], U32)

        cmp_c = sb("cmp_c", [P, experts, 32])
        counts = sb("counts", [P, experts])
        ntiles = sb("ntiles", [P, experts])
        cum_prod = sb("cum_prod", [P, experts, experts])
        cum = sb("cum", [P, experts])
        past = sb("past", [P, routed_tiles, experts])
        past_n = sb("past_n", [P, routed_tiles, experts])
        expert_f = sb("expert_f", [P, routed_tiles])
        first_f = sb("first_f", [P, routed_tiles])
        start_f = sb("start_f", [P, routed_tiles])
        expert_u = sb("expert_u", [P, routed_tiles], U32)
        start_u = sb("start_u", [P, routed_tiles], U32)
        pad_u = sb("pad_u", [P, experts], U32)
        pad_rows = sb("pad_rows", [P, ROW])

        xr = sb("xr", [P, RING, ROW])
        xrT = sb("xrT", [P, 2, KC, P])
        sgate = sb("sgate", [P, hidden])
        hid = sb("hid", [P, 2, hidden])
        hidT = sb("hidT", [P, HC, P])
        is_first = sb("is_first", [P, 1])
        w_row = sb("w_row", [P, 1])
        y = sb("y", [P, 2, dim])

        bank = [psum(f"bank{k}", [P, 512]) for k in range(8)]
        ps_scores = bank[0:4]
        ps_num, ps_state, ps_wo, ps_xnT = bank[0], bank[1], bank[2], bank[3]
        ps_qk, ps_xv, ps_qT, ps_small = bank[4], bank[5], bank[6], bank[7]

        weights_in = sem("weights_in")
        experts_in = sem("experts_in")
        x_loaded = [sem(f"x_loaded{u}") for u in range(RING)]
        acc_stored = [sem(f"acc_stored{u}") for u in range(RING)]
        scattered = [sem(f"scattered{u}") for u in range(RING)]
        pads_stored = sem("pads_stored")
        spare_zeroed = sem("spare_zeroed")
        init_done = sem("init_done")
        ln1_step = sem("ln1_step")
        mv1_ready = sem("mv1_ready")
        rstd1_ready = sem("rstd1_ready")
        xhat_ready = sem("xhat_ready")
        xhatT_psum = sem("xhatT_psum")
        xhatT_ready = sem("xhatT_ready")
        qk_psum = sem("qk_psum")
        v_psum = sem("v_psum")
        v_ready = sem("v_ready")
        rot_parts_ready = sem("rot_parts_ready")
        rot_ready = sem("rot_ready")
        exp_ready = sem("exp_ready")
        emin_ready = sem("emin_ready")
        phi_ready = sem("phi_ready")
        kcum_psum = sem("kcum_psum")
        kT_psum = sem("kT_psum")
        kT_ready = sem("kT_ready")
        kacc_ready = sem("kacc_ready")
        kcum_read = sem("kcum_read")
        den_step = sem("den_step")
        rden_ready = sem("rden_ready")
        qn_ready = sem("qn_ready")
        qT_psum = sem("qT_psum")
        qT_ready = sem("qT_ready")
        scores_psum = sem("scores_psum")
        attn_dve = sem("attn_dve")
        attn_copied = sem("attn_copied")
        attn_pool = sem("attn_pool")
        num_psum = sem("num_psum")
        yT_ready = sem("yT_ready")
        state_psum = sem("state_psum")
        state_add_ready = sem("state_add_ready")
        state_ready = sem("state_ready")
        wo_psum = sem("wo_psum")
        x1_ready = sem("x1_ready")
        ln2_step = sem("ln2_step")
        mv2_ready = sem("mv2_ready")
        pool_ln1_step = sem("pool_ln1_step")
        pool_ln2_step = sem("pool_ln2_step")
        rms2_ready = sem("rms2_ready")
        xhat2_ready = sem("xhat2_ready")
        xn_ready = sem("xn_ready")
        acc_ready = sem("acc_ready")
        tok_ready = sem("tok_ready")
        xnT_psum = sem("xnT_psum")
        xnT_ready = sem("xnT_ready")
        logits_psum = sem("logits_psum")
        ranks_psum = sem("ranks_psum")
        route_step = sem("route_step")
        members_ready = sem("members_ready")
        gap_ready = sem("gap_ready")
        egap_ready = sem("egap_ready")
        meta_ready = sem("meta_ready")
        macc_ready = sem("macc_ready")
        rank_step = sem("rank_step")
        slots_ready = sem("slots_ready")
        counts_psum = sem("counts_psum")
        table_step = sem("table_step")
        table_ready = sem("table_ready")
        rows_loaded = [sem(f"rows_loaded{u}") for u in range(RING)]
        xrT_psum = sem("xrT_psum")
        xrT_ready = sem("xrT_ready")
        gate_psum = sem("gate_psum")
        up_psum = sem("up_psum")
        sgate_ready = sem("sgate_ready")
        hid_ready = sem("hid_ready")
        hidT_psum = sem("hidT_psum")
        hidT_ready = sem("hidT_ready")
        down_psum = sem("down_psum")
        w_step = sem("w_step")
        y_ready = sem("y_ready")
        added = sem("added")

        block = ctx.enter_context(nc.Block())

        def alive(n):
            return not isinstance(n, int) or 0 <= n < tiles

        def over_tiles(eng, step):
            for n in range(-2, RING):
                step(n, n % RING)
            with eng.Fori(1, tiles // RING - 1) as group:
                for u in range(RING):
                    step(group * RING + u, u)
            for n in range(tiles - RING, tiles + 2):
                step(n, n % RING)

        ps_gate, ps_up = [bank[0], bank[1]], [bank[2], bank[3]]
        ps_xrT, ps_hidT, ps_down = bank[4], bank[5], [bank[6], bank[7]]

        def alive2(t):
            return not isinstance(t, int) or 0 <= t < routed_tiles

        def over_routed(eng, step):
            whole = routed_tiles // RING
            for t in range(-1, RING):
                step(t, t % RING)
            with eng.Fori(1, whole) as group:
                for u in range(RING):
                    step(group * RING + u, u)
            for t in range(whole * RING, routed_tiles + 1):
                step(t, t % RING)

        def settle(eng):
            eng.nop(nofuse=True)

        def first_round(n):
            return isinstance(n, int) and n < RING

        def later(n, k=1):
            return not isinstance(n, int) or n >= k

        @block.sync
        def _(sp):
            def x_rows(n, u):
                return bass.ds((u % 2) * length + (n // 2 if isinstance(n, int) else n_half(n, u)) * P, P)

            def n_half(n, u):
                return (n - (u % 2)) // 2

            def load_x(n, u):
                sp.dma_start(xin[:, u, :], x[x_rows(n, u), :]).then_inc(x_loaded[u], 16)

            for n in range(RING):
                load_x(n, n)
            sp.dma_start(cf[:, :], consts_f).then_inc(weights_in, 16)
            sp.dma_start(wqk_sb[:, :, :], w_qk.rearrange("(c p) n -> p c n", p=P)).then_inc(weights_in, 16)
            sp.dma_start(rope_sb[:, :, :], rope.rearrange("(i p) n -> p i n", p=P)).then_inc(weights_in, 16)
            sp.dma_start(ids[:, :], token_ids).then_inc(weights_in, 16)

            def step(n, u):
                if alive(n):
                    if not isinstance(n, int) or n + RING < tiles:
                        sp.wait_ge(x1_ready, n + 1)
                        load_x(n + RING, u)
                    sp.wait_ge(acc_ready, n + 1)
                    sp.dma_start(x_out[x_rows(n, u), :], acc[:, u, :]).then_inc(acc_stored[u], 16)

            over_tiles(sp, step)

            sp.wait_ge(table_ready, 1)
            for e in range(experts):
                at_row = sp.value_load(pad_u[0:1, e:e + 1], min_val=0, max_val=pad_region - P)
                sp.dma_start(routed_rows[bass.ds(at_row, P), :], pad_rows[:, :]).then_inc(pads_stored, 16)
            sp.dma_start(routed_rows[pad_region:pad_region + P, :], pad_rows[:, :]).then_inc(pads_stored, 16)
            sp.wait_ge(pads_stored, 16 * (experts + 1))
            for u in range(RING):
                sp.wait_ge(scattered[u], 32 * (tiles // RING))

            def load_rows(t, u):
                if not (isinstance(t, int) and t < RING):
                    sp.wait_ge(added, 16 * (t - RING + 1))
                start = sp.value_load(start_u[0:1, t:t + 1] if isinstance(t, int) else start_u[0:1, bass.ds(t, 1)],
                                      min_val=0, max_val=pad_region)
                sp.dma_start(xr[:, u, :], routed_rows[bass.ds(start, P), :]).then_inc(rows_loaded[u], 16)

            whole = routed_tiles // RING
            for t in range(RING):
                load_rows(t, t)
            with sp.Fori(1, whole) as group:
                for u in range(RING):
                    load_rows(group * RING + u, u)
            for t in range(whole * RING, routed_tiles):
                load_rows(t, t % RING)

        @block.scalar
        def _(act):
            act.dma_start(wv_sb[:, :, :], w_v.rearrange("(c p) n -> p c n", p=P)).then_inc(weights_in, 16)
            act.dma_start(wo_sb[:, :, :], w_o.rearrange("(c p) n -> p c n", p=P)).then_inc(weights_in, 16)
            act.dma_start(wr_sb[:, :, :], w_router.rearrange("(c p) n -> p c n", p=P)).then_inc(weights_in, 16)
            act.dma_start(cb[:, :], consts_b).then_inc(weights_in, 16)
            act.dma_start(scale_sb[:, :], norm_scale.to_broadcast([P, dim])).then_inc(weights_in, 16)
            for e in range(experts):
                act.dma_start(up_sb[:, e, :], w_up[:, e, :]).then_inc(experts_in, 16)
                act.dma_start(down_sb[:, e, :], w_down[:, e, :]).then_inc(experts_in, 16)
            act.wait_ge(weights_in, 16 * 9)
            act.wait_ge(init_done, 1)

            def step(n, u):
                b, nb = u % 2, (u + 1) % 2
                m = n + 1
                if alive(m):
                    act.wait_ge(xhatT_psum, m + 1)
                    nc.scalar.activation(xhatT[:, nb, :, :], ps_xv[:, 0:dim], ACT.Copy).then_inc(xhatT_ready, 1)
                if alive(n):
                    if later(n):
                        act.wait_ge(num_psum, n)
                    act.wait_ge(scores_psum, 4 * n + 4)
                    nc.scalar.activation(attn[:, 3, :, :, :], ps_scores[3][:, :], ACT.Copy).then_inc(attn_copied, 1)
                if alive(m):
                    act.wait_ge(v_psum, m + 1)
                    if later(m, 2):
                        act.wait_ge(state_psum, m - 1)
                    nc.scalar.activation(
                        v_pad[:, nb, :, :].rearrange("p (a b) (c d) -> p a (b c) d", b=2, c=2)[:, :, 0:4:3, :],
                        ps_xv[:, dim:2 * dim], ACT.Copy).then_inc(v_ready, 1)
                    act.wait_ge(rot_ready, m + 1)
                    if later(m):
                        act.wait_ge(emin_ready, m)
                    nc.scalar.activation(erot[:, :], rot[:, :], ACT.Exp).then_inc(exp_ready, 1)
                if alive(n):
                    act.wait_ge(num_psum, n + 1)
                    if later(n):
                        act.wait_ge(wo_psum, n)
                    nc.scalar.activation(yT[:, :, :], ps_num[:, 0:dim], ACT.Copy).then_inc(yT_ready, 1)
                if alive(m):
                    act.wait_ge(kT_psum, m + 1)
                    nc.scalar.activation(kT[:, :, :], ps_xv[:, 0:dim], ACT.Copy).then_inc(kT_ready, 1)
                if alive(n - 1):
                    act.wait_ge(xnT_psum, n)
                    if later(n - 1):
                        act.wait_ge(logits_psum, n - 1)
                    nc.scalar.activation(xnT[:, :, :], ps_xnT[:, 0:dim], ACT.Copy).then_inc(xnT_ready, 1)
                if alive(m):
                    act.wait_ge(qT_psum, m + 1)
                    nc.scalar.activation(qT[:, :, :], ps_qT[:, 0:dim], ACT.Copy).then_inc(qT_ready, 1)
                    for par in range(2):
                        nc.scalar.activation(q_par[:, :, par, :],
                                             ps_qT[:, 0:dim].rearrange("p (c t) -> p c t", c=KC),
                                             ACT.Copy, scale=parity_mask[:, par:par + 1]).then_inc(qT_ready, 1)
                if alive(n - 1):
                    act.wait_ge(gap_ready, n)
                    nc.scalar.activation(egap[:, :], gap[:, :], ACT.Exp).then_inc(egap_ready, 1)

            over_tiles(act, step)

            def gate(t):
                act.wait_ge(gate_psum, t + 1)
                if not (isinstance(t, int) and t < 1):
                    act.wait_ge(hid_ready, t)
                return act

            def step2(t, u):
                b = u % 2
                if alive2(t + 1):
                    act.wait_ge(xrT_psum, t + 2)
                    nc.scalar.activation(xrT[:, 1 - b, :, :], ps_xrT[:, 0:dim], ACT.Copy).then_inc(xrT_ready, 1)
                if alive2(t - 1):
                    act.wait_ge(hidT_psum, t)
                    nc.scalar.activation(hidT[:, :, :], ps_hidT[:, :], ACT.Copy).then_inc(hidT_ready, 1)
                if alive2(t):
                    gate(t)
                    nc.scalar.activation(sgate[:, :], ps_gate[b][:, :], ACT.Silu).then_inc(sgate_ready, 1)

            over_routed(act, step2)

        @block.vector
        def _(dve):
            nc.vector.memset(v_pad[:, :, :, :], 0.0).then_inc(init_done, 1)
            nc.vector.memset(pad_rows[:, :], 0.0).then_inc(table_step, 1)
            dve.wait_ge(weights_in, 16 * 9)
            dve.wait_ge(table_step, 1)
            nc.vector.tensor_copy(pad_rows[:, TOKEN:TOKEN + 1].bitcast(U32), ids[:, tiles:tiles + 1]).then_inc(table_step, 1)

            def ln1(n, u):
                b = u % 2
                s = Steps(dve, ln1_step, n, 1)
                dve.wait_ge(x_loaded[u], 16 * (n // RING if isinstance(n, int) else (n - u) // RING) + 16)
                s.done(nc.vector.bn_stats(stats1[:, b, :], xin[:, u, :]))
                if later(n, 2):
                    dve.wait_ge(rstd1_ready, n - 1)
                settle(dve)
                nc.vector.bn_aggr(mv1[:, b, :], stats1[:, b, :]).then_inc(mv1_ready, 1)
                s.close()

            def norm1(n, u):
                b = u % 2
                dve.wait_ge(rstd1_ready, n + 1)
                dve.wait_ge(mv1_ready, n + 1)
                if later(n, 2):
                    dve.wait_ge(xhatT_psum, n - 1)
                nc.vector.tensor_scalar(xhat[:, b, :], xin[:, u, :], mv1[:, b, 0:1], rstd1[:, b, :],
                                        ALU.subtract, ALU.mult).then_inc(xhat_ready, 1)

            def masks(n, u):
                if later(n):
                    dve.wait_ge(num_psum, n)
                for g in range(3):
                    dve.wait_ge(scores_psum, 4 * n + g + 1)
                    nc.vector.tensor_tensor(attn[:, g, :, :, :].rearrange("p c a t -> p (c a) t"),
                                            ps_scores[g][:, :].rearrange("p (h t) -> p h t", h=4),
                                            causal.unsqueeze(1).to_broadcast([P, 4, P]),
                                            ALU.mult).then_inc(attn_dve, 1)

            def rotate(n, u):
                i = n // 2 if isinstance(n, int) else (n - u % 2) // 2
                table = rope_sb[:, bass.ds(i, 1), :].rearrange("p i n -> p (i n)")
                cos = table[:, 0:HEAD_DIM].unsqueeze(1).to_broadcast([P, 2 * heads, HEAD_DIM])
                dve.wait_ge(qk_psum, n + 1)
                if later(n):
                    dve.wait_ge(rot_ready, n)
                qk = ps_qk[:, :].rearrange("p (h d) -> p h d", d=HEAD_DIM)
                half = HEAD_DIM // 2
                nc.vector.tensor_tensor(rot_a[:, :].rearrange("p (h d) -> p h d", d=HEAD_DIM), qk, cos,
                                        ALU.mult).then_inc(rot_parts_ready, 1)
                rb = rot_b[:, :].rearrange("p (h d) -> p h d", d=HEAD_DIM)
                for k in range(2):
                    sin = table[:, HEAD_DIM + k * half:HEAD_DIM + (k + 1) * half].unsqueeze(1)
                    nc.vector.tensor_tensor(rb[:, :, k * half:(k + 1) * half],
                                            qk[:, :, (1 - k) * half:(2 - k) * half],
                                            sin.to_broadcast([P, 2 * heads, half]),
                                            ALU.mult).then_inc(rot_parts_ready, 1)

            def features(n, u):
                b = u % 2
                dve.wait_ge(emin_ready, n + 1)
                if later(n, 2):
                    dve.wait_ge(state_psum, n - 1)
                nc.vector.scalar_tensor_tensor(phi[:, b, :], rot[:, :], 1.0, emin[:, :], ALU.add,
                                               ALU.max).then_inc(phi_ready, 1)

            def state_part(n, u):
                dve.wait_ge(state_psum, n + 1)
                if later(n):
                    dve.wait_ge(state_ready, n)
                nc.vector.tensor_tensor(state_add[:, :, :],
                                        ps_state[:, 0:dim].rearrange("p (c t) -> p c t", c=KC),
                                        same_head.unsqueeze(1).to_broadcast([P, KC, P]),
                                        ALU.mult).then_inc(state_add_ready, 1)

            def denominators(n, u):
                b = u % 2
                s = Steps(dve, den_step, n, 2)
                dve.wait_ge(kcum_psum, n + 1)
                dve.wait_ge(phi_ready, n + 1)
                nc.vector.tensor_tensor(qk_prod[:, :], ps_small[:, 0:dim], phi[:, b, 0:dim],
                                        ALU.mult).then_inc(kcum_read, 1)
                dve.wait_ge(kcum_read, n + 1)
                s.done(nc.vector.tensor_reduce(den[:, :], qk_prod[:, :].rearrange("p (h d) -> p h d", d=HEAD_DIM),
                                               AX_X, ALU.add))
                s.done(nc.vector.tensor_scalar(den[:, :], den[:, :], DEN_EPS, None, ALU.max))
                if later(n):
                    dve.wait_ge(qn_ready, n)
                nc.vector.reciprocal(rden[:, :], den[:, :]).then_inc(rden_ready, 1)
                s.close()

            def residual(n, u):
                s = Steps(dve, ln2_step, n, 1)
                dve.wait_ge(wo_psum, n + 1)
                if later(n):
                    dve.wait_ge(acc_ready, n)
                    dve.wait_ge(xhat2_ready, n)
                nc.vector.tensor_tensor(x1[:, :], ps_wo[:, 0:dim], xin[:, u, :], ALU.add).then_inc(x1_ready, 1)
                dve.wait_ge(x1_ready, n + 1)
                s.done(nc.vector.bn_stats(stats2[:, :], x1[:, :]))
                if later(n):
                    dve.wait_ge(rms2_ready, n)
                settle(dve)
                nc.vector.bn_aggr(mv2[:, :], stats2[:, :]).then_inc(mv2_ready, 1)
                s.close()

            def norm2(n, u):
                dve.wait_ge(rms2_ready, n + 1)
                dve.wait_ge(mv2_ready, n + 1)
                nc.vector.tensor_scalar(xhat2[:, :], x1[:, :], mv2[:, 0:1], rstd2[:, :],
                                        ALU.subtract, ALU.mult).then_inc(xhat2_ready, 1)
                dve.wait_ge(xhat2_ready, n + 1)
                if not first_round(n):
                    dve.wait_ge(scattered[u], 8 * (n - u))
                nc.vector.scalar_tensor_tensor(rows[:, u, 0:dim], xhat2[:, :], rms2[:, :], scale_sb[:, :],
                                               ALU.mult, ALU.mult).then_inc(xn_ready, 1)

            def route(n, u):
                b = u % 2
                s = Steps(dve, route_step, n, 7)
                dve.wait_ge(logits_psum, n + 1)
                s.done(nc.vector.tensor_copy(scores8[:, :], ps_small[:, 256:256 + experts]))
                settle(dve)
                s.done(nc.vector.max(top8[:, :], scores8[:, :]))
                if later(n):
                    dve.wait_ge(egap_ready, n)
                nc.vector.tensor_tensor(gap[:, :], top8[:, 1:2], top8[:, 0:1], ALU.subtract).then_inc(gap_ready, 1)
                s.done(nc.vector.max_index(top8_at[:, :], top8[:, :], scores8[:, :]))
                s.done(nc.vector.tensor_copy(chosen[:, b, :], top8_at[:, 0:2]))
                s.done(nc.vector.tensor_tensor(
                    onehot[:, b, :, :], expert_iota.unsqueeze(1).to_broadcast([P, 2, experts]),
                    chosen[:, b, :].unsqueeze(2).to_broadcast([P, 2, experts]), ALU.is_equal))
                if later(n, 2):
                    dve.wait_ge(macc_ready, n - 1)
                    dve.wait_ge(ranks_psum, n - 1)
                nc.vector.tensor_tensor(members[:, b, :], onehot[:, b, 0, :], onehot[:, b, 1, :],
                                        ALU.add).then_inc(members_ready, 1)
                dve.wait_ge(egap_ready, n + 1)
                s.done(nc.vector.tensor_scalar(gap1[:, :], egap[:, :], 1.0, None, ALU.add))
                s.done(nc.vector.reciprocal(w_first[:, :], gap1[:, :]))
                nc.vector.tensor_tensor(rows[:, u, W_SECOND:W_SECOND + 1], w_first[:, :], egap[:, :],
                                        ALU.mult).then_inc(meta_ready, 1)
                nc.vector.tensor_copy(rows[:, u, FIRST_EXPERT:FIRST_EXPERT + 1], chosen[:, b, 0:1]).then_inc(meta_ready, 1)
                dve.wait_ge(meta_ready, 3 * n + 1)
                nc.vector.tensor_tensor(rows[:, u, W_GAP:W_GAP + 1], w_first[:, :],
                                        rows[:, u, W_SECOND:W_SECOND + 1], ALU.subtract).then_inc(meta_ready, 1)
                s.close()

            def places(n, u):
                b = u % 2
                s = Steps(dve, rank_step, n, 2)
                dve.wait_ge(ranks_psum, n + 1)
                if not isinstance(n, int) or n + 1 < tiles:
                    dve.wait_ge(logits_psum, n + 2)
                s.done(nc.vector.tensor_tensor(
                    rank_prod[:, :, :], ps_small[:, 264:264 + experts].unsqueeze(1).to_broadcast([P, 2, experts]),
                    onehot[:, b, :, :], ALU.mult))
                s.done(nc.vector.tensor_reduce(rank[:, :], rank_prod[:, :, :], AX_X, ALU.add))
                if later(n, 2):
                    dve.wait_ge(scattered[(u + 2) % RING], 8 * (n - 2 - (u + 2) % RING) + 32)
                nc.vector.scalar_tensor_tensor(slot_of[:, b, :], chosen[:, b, :], float(region), rank[:, :],
                                               ALU.mult, ALU.add).then_inc(slots_ready, 1)
                s.close()

            def step(n, u):
                m, um = n + 1, (u + 1) % RING
                if alive(n + 2):
                    ln1(n + 2, (u + 2) % RING)
                if alive(n):
                    masks(n, u)
                if alive(m):
                    rotate(m, um)
                if alive(n + 2):
                    norm1(n + 2, (u + 2) % RING)
                if alive(m):
                    features(m, um)
                if alive(n):
                    state_part(n, u)
                if alive(m):
                    denominators(m, um)
                if alive(n):
                    residual(n, u)
                if alive(n - 2):
                    places(n - 2, (u + 2) % RING)
                if alive(n - 1):
                    route(n - 1, (u + 3) % RING)
                if alive(n):
                    norm2(n, u)

            over_tiles(dve, step)

            done = [2]

            def link(ins):
                done[0] += 1
                ins.then_inc(table_step, 1)
                dve.wait_ge(table_step, done[0])

            NT = routed_tiles
            dve.wait_ge(counts_psum, 1)
            link(nc.vector.tensor_copy(counts[:, :], ps_small[:, 272:272 + experts]))
            link(nc.vector.tensor_tensor(cmp_c[:, :, :], counts[:, :].unsqueeze(2).to_broadcast([P, experts, 32]),
                                         tile_starts.unsqueeze(1).to_broadcast([P, experts, 32]), ALU.is_gt))
            link(nc.vector.tensor_reduce(ntiles[:, :], cmp_c[:, :, :], AX_X, ALU.add))
            link(nc.vector.tensor_tensor(cum_prod[:, :, :], low_tri.rearrange("p (e f) -> p e f", e=experts),
                                         ntiles[:, :].unsqueeze(1).to_broadcast([P, experts, experts]), ALU.mult))
            link(nc.vector.tensor_reduce(cum[:, :], cum_prod[:, :, :], AX_X, ALU.add))
            link(nc.vector.tensor_tensor(past[:, :, :], tile_iota.unsqueeze(2).to_broadcast([P, NT, experts]),
                                         cum[:, :].unsqueeze(1).to_broadcast([P, NT, experts]), ALU.is_ge))
            link(nc.vector.tensor_reduce(expert_f[:, :], past[:, :, :], AX_X, ALU.add))
            link(nc.vector.tensor_tensor(past_n[:, :, :], past[:, :, :],
                                         ntiles[:, :].unsqueeze(1).to_broadcast([P, NT, experts]), ALU.mult))
            link(nc.vector.tensor_reduce(first_f[:, :], past_n[:, :, :], AX_X, ALU.add))
            link(nc.vector.tensor_tensor(start_f[:, :], tile_iota, first_f[:, :], ALU.subtract))
            link(nc.vector.tensor_scalar(start_f[:, :], start_f[:, :], float(P), None, ALU.mult))
            link(nc.vector.scalar_tensor_tensor(start_f[:, :], expert_f[:, :], float(region), start_f[:, :],
                                                ALU.mult, ALU.add))
            link(nc.vector.tensor_scalar(start_u[:, :], start_f[:, :], float(pad_region), None, ALU.min))
            link(nc.vector.tensor_scalar(expert_f[:, :], expert_f[:, :], float(experts - 1), None, ALU.min))
            link(nc.vector.tensor_copy(expert_u[:, :], expert_f[:, :]))
            nc.vector.tensor_tensor(pad_u[:, :], region_start, counts[:, :], ALU.add).then_inc(table_ready, 1)

            def hidden_product(t, u):
                b = u % 2
                dve.wait_ge(up_psum, t + 1)
                dve.wait_ge(sgate_ready, t + 1)
                if not (isinstance(t, int) and t < 2):
                    dve.wait_ge(hidT_psum, t - 1)
                nc.vector.tensor_tensor(hid[:, b, :], ps_up[b][:, :], sgate[:, :], ALU.mult).then_inc(hid_ready, 1)

            def weigh(t, u):
                b = u % 2
                s = Steps(dve, w_step, t, 2)
                dve.wait_ge(rows_loaded[u], 4 * (t - u) + 16)
                e_t = expert_f[:, t:t + 1] if isinstance(t, int) else expert_f[:, bass.ds(t, 1)]
                s.done(nc.vector.tensor_tensor(is_first[:, :], xr[:, u, FIRST_EXPERT:FIRST_EXPERT + 1], e_t, ALU.is_equal))
                s.done(nc.vector.scalar_tensor_tensor(w_row[:, :], is_first[:, :], xr[:, u, W_GAP:W_GAP + 1],
                                                      xr[:, u, W_SECOND:W_SECOND + 1], ALU.mult, ALU.add))
                dve.wait_ge(down_psum, t + 1)
                if not (isinstance(t, int) and t < 2):
                    dve.wait_ge(added, 16 * (t - 1))
                nc.vector.tensor_scalar(y[:, b, :], ps_down[b][:, 0:dim], w_row[:, :], None,
                                        ALU.mult).then_inc(y_ready, 1)
                s.close()

            def step2(t, u):
                if alive2(t):
                    hidden_product(t, u)
                if alive2(t - 1):
                    weigh(t - 1, (u + 3) % RING)

            over_routed(dve, step2)

        @block.gpsimd
        def _(pool):
            nc.gpsimd.memset(state[:, :, :, :], 0.0).then_inc(init_done, 1)
            nc.gpsimd.memset(kacc[:, :, :], 0.0).then_inc(init_done, 1)
            nc.gpsimd.memset(macc[:, :], 0.0).then_inc(init_done, 1)
            pool.wait_ge(init_done, 4)
            pool.wait_ge(weights_in, 16 * 9)
            pool.wait_ge(table_step, 2)
            pool.dma_start(out[tokens:tokens + P, :], pad_rows[:, 0:dim]).then_inc(spare_zeroed, 16)

            def rstd_first(n, u):
                b = u % 2
                pool.wait_ge(mv1_ready, n + 1)
                if later(n, 2):
                    pool.wait_ge(xhat_ready, n - 1)
                s = Steps(pool, pool_ln1_step, n, 1)
                settle(pool)
                s.done(nc.gpsimd.tensor_scalar(var1[:, :], mv1[:, b, 1:2], LN_EPS, None, ALU.add))
                nc.gpsimd.tensor_tensor(rstd1[:, b, :], var1[:, :], minus_half, ALU.pow).then_inc(rstd1_ready, 1)
                s.close()

            def rotated(n, u):
                pool.wait_ge(rot_parts_ready, 3 * n + 3)
                if later(n):
                    pool.wait_ge(phi_ready, n)
                nc.gpsimd.tensor_tensor(rot[:, :], rot_a[:, :], rot_b[:, :], ALU.add).then_inc(rot_ready, 1)

            def clamp(n, u):
                pool.wait_ge(exp_ready, n + 1)
                if later(n):
                    pool.wait_ge(phi_ready, n)
                settle(pool)
                nc.gpsimd.tensor_scalar(emin[:, :], erot[:, :], 1.0, None, ALU.min).then_inc(emin_ready, 1)

            def mask(n, u):
                pool.wait_ge(attn_copied, n + 1)
                part = attn[:, 3, :, :, :].rearrange("p c a t -> p (c a) t")
                nc.gpsimd.tensor_tensor(part, part, causal.unsqueeze(1).to_broadcast([P, 4, P]),
                                        ALU.mult).then_inc(attn_pool, 1)

            def state_sum(n, u):
                b = u % 2
                pool.wait_ge(state_add_ready, n + 1)
                pool.wait_ge(num_psum, n + 1)
                if later(n, 2):
                    pool.wait_ge(state_ready, n - 1)
                nc.gpsimd.tensor_tensor(state[:, b, :, :], state[:, b, :, :], state_add[:, :, :],
                                        ALU.add).then_inc(state_ready, 1)

            def key_sum(n, u):
                b = u % 2
                pool.wait_ge(kcum_psum, n + 1)
                pool.wait_ge(phi_ready, n + 1)
                if later(n, 2):
                    pool.wait_ge(kacc_ready, n - 1)
                nc.gpsimd.tensor_tensor(kacc[:, b, :], kacc[:, b, :], phi[:, b, dim:2 * dim],
                                        ALU.add).then_inc(kacc_ready, 1)

            def scale_q(n, u):
                b = u % 2
                pool.wait_ge(rden_ready, n + 1)
                if later(n):
                    pool.wait_ge(qT_psum, n)
                nc.gpsimd.tensor_tensor(qn[:, :].rearrange("p (h d) -> p h d", d=HEAD_DIM),
                                        phi[:, b, 0:dim].rearrange("p (h d) -> p h d", d=HEAD_DIM),
                                        rden[:, :].unsqueeze(2).to_broadcast([P, heads, HEAD_DIM]),
                                        ALU.mult).then_inc(qn_ready, 1)

            def norm2_scales(n, u):
                s = Steps(pool, pool_ln2_step, n, 4)
                pool.wait_ge(mv2_ready, n + 1)
                if later(n):
                    pool.wait_ge(xn_ready, n)
                settle(pool)
                s.done(nc.gpsimd.tensor_scalar(var2[:, :], mv2[:, 1:2], LN_EPS, None, ALU.add))
                s.done(nc.gpsimd.tensor_tensor(rstd2[:, :], var2[:, :], minus_half, ALU.pow))
                settle(pool)
                s.done(nc.gpsimd.tensor_scalar(ms2[:, :], rstd2[:, :], rstd2[:, :], mv2[:, 1:2], ALU.mult, ALU.mult))
                settle(pool)
                s.done(nc.gpsimd.tensor_scalar(ms2[:, :], ms2[:, :], RMS_EPS, None, ALU.add))
                nc.gpsimd.tensor_tensor(rms2[:, :], ms2[:, :], minus_half, ALU.pow).then_inc(rms2_ready, 1)
                s.close()

            def accumulate(n, u):
                pool.wait_ge(xhat2_ready, n + 1)
                if not first_round(n):
                    pool.wait_ge(acc_stored[u], 4 * (n - u))
                nc.gpsimd.tensor_tensor(acc[:, u, :], x1[:, :], xhat2[:, :], ALU.add).then_inc(acc_ready, 1)

            def token_column(n, u):
                if not first_round(n):
                    pool.wait_ge(scattered[u], 8 * (n - u))
                nc.gpsimd.tensor_copy(rows[:, u, TOKEN:TOKEN + 1].bitcast(U32),
                                      ids[:, n:n + 1] if isinstance(n, int) else ids[:, bass.ds(n, 1)]).then_inc(tok_ready, 1)

            def member_sum(n, u):
                b = u % 2
                pool.wait_ge(ranks_psum, n + 1)
                pool.wait_ge(members_ready, n + 1)
                if later(n):
                    pool.wait_ge(macc_ready, n)
                nc.gpsimd.tensor_tensor(macc[:, :], macc[:, :], members[:, b, :], ALU.add).then_inc(macc_ready, 1)

            def scatter(n, u):
                b = u % 2
                pool.wait_ge(slots_ready, n + 1)
                pool.wait_ge(meta_ready, 3 * n + 3)
                pool.wait_ge(xn_ready, n + 1)
                pool.wait_ge(tok_ready, n + 1)
                settle(pool)
                for k in range(2):
                    pool.indirect_dma_start(out=routed_rows[:, :],
                                            out_offset=bass.IndirectOffsetOnAxis(ap=slot_of[:, b, k:k + 1], axis=0),
                                            in_=rows[:, u, :], in_offset=None).then_inc(scattered[u], 16)

            def step(n, u):
                m, um = n + 1, (u + 1) % RING
                if alive(n + 2):
                    rstd_first(n + 2, (u + 2) % RING)
                if alive(n):
                    mask(n, u)
                if alive(m):
                    rotated(m, um)
                    clamp(m, um)
                if alive(n):
                    state_sum(n, u)
                if alive(m):
                    key_sum(m, um)
                    scale_q(m, um)
                if alive(n):
                    norm2_scales(n, u)
                if alive(n - 2):
                    member_sum(n - 2, (u + 2) % RING)
                    scatter(n - 2, (u + 2) % RING)
                if alive(n):
                    accumulate(n, u)
                    token_column(n, u)

            over_tiles(pool, step)

            for u in range(RING):
                pool.wait_ge(acc_stored[u], 16 * (tiles // RING))
            pool.wait_ge(spare_zeroed, 16)

            def step2(t, u):
                if not alive2(t - 1):
                    return
                t, u = t - 1, (u + 3) % RING
                pool.wait_ge(y_ready, t + 1)
                if not (isinstance(t, int) and t < 1):
                    pool.wait_ge(added, 16 * t)
                settle(pool)
                pool.indirect_dma_start(
                    out=out[:, :], out_offset=bass.IndirectOffsetOnAxis(ap=xr[:, u, TOKEN:TOKEN + 1].bitcast(U32), axis=0),
                    in_=y[:, u % 2, :], in_offset=None, compute_op=ALU.add).then_inc(added, 16)

            over_routed(pool, step2)
            pool.wait_ge(added, 16 * routed_tiles)

        @block.tensor
        def _(pe):
            pe.wait_ge(weights_in, 16 * 9)
            pe.wait_ge(init_done, 4)

            def transposes(dst, src, chunks):
                for c in range(chunks):
                    last = nc.tensor.transpose(dst[:, c * P:(c + 1) * P], src[:, c * P:(c + 1) * P], ident)
                return last

            def product(dst, lhs, rhs, chunks):
                for c in range(chunks):
                    last = nc.tensor.matmul(dst, lhs(c), rhs(c), start=c == 0, stop=c == chunks - 1)
                return last

            def transpose_x(n, u):
                pe.wait_ge(xhat_ready, n + 1)
                if later(n):
                    pe.wait_ge(kT_ready, n)
                transposes(ps_xv, xhat[:, u % 2, :], KC).then_inc(xhatT_psum, 1)

            def scores(n, u):
                pe.wait_ge(qT_ready, 3 * n + 3)
                pe.wait_ge(kT_ready, n + 1)
                if later(n):
                    pe.wait_ge(yT_ready, n)
                    pe.wait_ge(state_add_ready, n)
                    pe.wait_ge(x1_ready, n)
                if later(n, 2):
                    pe.wait_ge(xnT_ready, n - 1)
                for g in range(4):
                    rows32 = slice(32 * g, 32 * g + 32)
                    for c in range(KC):
                        last = nc.tensor.matmul(ps_scores[g][:, c * 2 * P:(c + 1) * 2 * P], kT[rows32, c, :],
                                                q_par[rows32, c, :, :].rearrange("p a t -> p (a t)"),
                                                start=True, stop=True)
                    last.then_inc(scores_psum, 1)

            def project(n, u):
                b = u % 2
                pe.wait_ge(xhatT_ready, n + 1)
                if later(n):
                    pe.wait_ge(rot_parts_ready, 3 * n)
                product(ps_qk[:, :], lambda c: xhatT[:, b, c, :], lambda c: wqk_sb[:, c, :], KC).then_inc(qk_psum, 1)
                product(ps_xv[:, dim:2 * dim], lambda c: xhatT[:, b, c, :], lambda c: wv_sb[:, c, :], KC).then_inc(v_psum, 1)

            def v_of(b, c):
                v = v_pad[:, b, 8 * c:8 * c + 8, :].rearrange("p (a b) (c d) -> p a (b c) d", b=2, c=2)
                return v[:, :, 0:4:3, :]

            def attend(n, u):
                b = u % 2
                pe.wait_ge(attn_dve, 3 * n + 3)
                pe.wait_ge(attn_pool, n + 1)
                pe.wait_ge(v_ready, n + 1)
                if later(n, 2):
                    pe.wait_ge(state_ready, n - 1)
                for c in range(KC):
                    nc.tensor.matmul(ps_num[:, c * P:(c + 1) * P], state[:, b, c, :], qT[:, c, :],
                                     start=c == 0, stop=False, skip_group_check=True)
                for c in range(KC):
                    for par in range(2):
                        for g in range(4):
                            last = nc.tensor.matmul(ps_num[32 * g:32 * g + 32, c * P:(c + 1) * P],
                                                    v_pad[:, b, 8 * c + 2 * g + par, :], attn[:, g, c, par, :],
                                                    start=False, stop=c == KC - 1 and par == 1, skip_group_check=True)
                last.then_inc(num_psum, 1)
                for c in range(KC):
                    last = nc.tensor.matmul(ps_state[:, c * P:(c + 1) * P], phi[:, b, dim + c * P:dim + (c + 1) * P],
                                            v_of(b, c), start=True, stop=True)
                last.then_inc(state_psum, 1)

            def key_prefix(n, u):
                b = u % 2
                pe.wait_ge(phi_ready, n + 1)
                if later(n, 2):
                    pe.wait_ge(kacc_ready, n - 1)
                small_free(n)
                k = phi[:, b, dim:2 * dim]
                nc.tensor.matmul(ps_small[:, 0:dim], causal, k, start=True, stop=False)
                nc.tensor.matmul(ps_small[:, 0:dim], ones, kacc[:, b, :], start=False, stop=True).then_inc(kcum_psum, 1)
                pe.wait_ge(v_ready, n + 1)
                transposes(ps_xv, k, KC).then_inc(kT_psum, 1)

            def small_free(m):
                if later(m, 3):
                    pe.wait_ge(route_step, 7 * (m - 3) + 1)
                if later(m, 4):
                    pe.wait_ge(rank_step, 2 * (m - 4) + 1)

            def output_projection(n, u):
                pe.wait_ge(yT_ready, n + 1)
                product(ps_wo[:, 0:dim], lambda c: yT[:, c, :], lambda c: wo_sb[:, c, :], KC).then_inc(wo_psum, 1)

            def transpose_xn(n, u):
                pe.wait_ge(xn_ready, n + 1)
                transposes(ps_xnT, rows[:, u, 0:dim], KC).then_inc(xnT_psum, 1)

            def logits(n, u):
                pe.wait_ge(xnT_ready, n + 1)
                product(ps_small[:, 256:256 + experts], lambda c: xnT[:, c, :], lambda c: wr_sb[:, c, :], KC).then_inc(logits_psum, 1)

            def ranks(n, u):
                pe.wait_ge(members_ready, n + 1)
                if later(n):
                    pe.wait_ge(macc_ready, n)
                nc.tensor.matmul(ps_small[:, 264:264 + experts], earlier, members[:, u % 2, :], start=True, stop=False)
                nc.tensor.matmul(ps_small[:, 264:264 + experts], ones_b, macc[:, :], start=False, stop=True).then_inc(ranks_psum, 1)

            def transpose_q(n, u):
                pe.wait_ge(qn_ready, n + 1)
                if later(n):
                    pe.wait_ge(qT_ready, 3 * n)
                transposes(ps_qT, qn[:, :], KC).then_inc(qT_psum, 1)

            def step(n, u):
                m, um = n + 1, (u + 1) % RING
                if alive(m):
                    transpose_x(m, um)
                if alive(n):
                    scores(n, u)
                if alive(m):
                    project(m, um)
                if alive(n):
                    attend(n, u)
                if alive(m):
                    key_prefix(m, um)
                if alive(n - 1):
                    transpose_xn(n - 1, (u + 3) % RING)
                if alive(n):
                    output_projection(n, u)
                if alive(m):
                    pe.wait_ge(kcum_read, m + 1)
                if alive(n - 2):
                    ranks(n - 2, (u + 2) % RING)
                if alive(n - 1):
                    logits(n - 1, (u + 3) % RING)
                if alive(m):
                    transpose_q(m, um)

            over_tiles(pe, step)

            pe.wait_ge(macc_ready, tiles)
            pe.wait_ge(rank_step, 2 * tiles - 1)
            pe.wait_ge(route_step, 7 * tiles - 6)
            nc.tensor.matmul(ps_small[:, 272:272 + experts], ones_b, macc[:, :], start=True, stop=True).then_inc(counts_psum, 1)

            pe.wait_ge(experts_in, 16 * 2 * experts)
            pe.wait_ge(table_ready, 1)

            def transpose_rows(t, u):
                pe.wait_ge(rows_loaded[u], 4 * (t - u) + 16)
                if not (isinstance(t, int) and t < 1):
                    pe.wait_ge(xrT_ready, t)
                transposes(ps_xrT, xr[:, u, 0:dim], KC).then_inc(xrT_psum, 1)

            def expert_of(t):
                return pe.value_load(expert_u[0:1, t:t + 1] if isinstance(t, int) else expert_u[0:1, bass.ds(t, 1)],
                                     min_val=0, max_val=experts - 1)

            def up(t, u):
                b = u % 2
                e = expert_of(t)
                pe.wait_ge(xrT_ready, t + 1)
                if not (isinstance(t, int) and t < 2):
                    pe.wait_ge(sgate_ready, t - 1)
                    pe.wait_ge(hid_ready, t - 1)
                for half, (dst, signal) in enumerate([(ps_up, up_psum), (ps_gate, gate_psum)][::-1]):
                    at0 = hidden * (1 - half)
                    for c in range(KC):
                        w = up_sb[:, bass.ds(e, 1), c * 2 * hidden + at0:c * 2 * hidden + at0 + hidden]
                        last = nc.tensor.matmul(dst[b][:, :], xrT[:, b, c, :], w.rearrange("p e n -> p (e n)"),
                                                start=c == 0, stop=c == KC - 1)
                    last.then_inc(signal, 1)

            def transpose_hidden(t, u):
                pe.wait_ge(hid_ready, t + 1)
                if not (isinstance(t, int) and t < 1):
                    pe.wait_ge(hidT_ready, t)
                transposes(ps_hidT, hid[:, u % 2, :], HC).then_inc(hidT_psum, 1)

            def down(t, u):
                b = u % 2
                e = expert_of(t)
                pe.wait_ge(hidT_ready, t + 1)
                if not (isinstance(t, int) and t < 2):
                    pe.wait_ge(y_ready, t - 1)
                for c in range(HC):
                    w = down_sb[:, bass.ds(e, 1), c * dim:(c + 1) * dim]
                    last = nc.tensor.matmul(ps_down[b][:, 0:dim], hidT[:, c, :], w.rearrange("p e n -> p (e n)"),
                                            start=c == 0, stop=c == HC - 1)
                last.then_inc(down_psum, 1)

            def step2(t, u):
                if alive2(t + 1):
                    transpose_rows(t + 1, (u + 1) % RING)
                if alive2(t - 1):
                    transpose_hidden(t - 1, (u + 3) % RING)
                if alive2(t):
                    up(t, u)
                if alive2(t - 1):
                    down(t - 1, (u + 3) % RING)

            over_routed(pe, step2)


_B, _T, _D, _E, _H = 2, 2048, 256, 8, 512


def kernel(**inputs):
    import numpy as np
    import concourse.bacc as bacc
    from concourse.bass_utils import run_bass_kernel_spmd

    f32 = np.float32
    tokens, tiles, region, routed = sizes(_B, _T, _D, _E, _H)

    def arr(name):
        return np.asarray(inputs[name])

    half = HEAD_DIM // 2
    inv_freq = f32(10000.0) ** (-np.arange(half, dtype=f32) / f32(half))
    angle = np.arange(_T, dtype=f32)[:, None] * inv_freq.astype(f32)[None, :]
    cos, sin = np.cos(angle), np.sin(angle)
    s, t = np.arange(P)[:, None], np.arange(P)[None, :]
    rep = lambda row: np.broadcast_to(np.asarray(row, f32).reshape(1, -1), (P, np.asarray(row).size))
    parity = (np.arange(P)[:, None] // HEAD_DIM) % 2 == np.arange(2)[None, :]
    consts_f = np.concatenate([
        s == t, s <= t, np.ones((P, P)), s // HEAD_DIM == t // HEAD_DIM, parity,
        rep(np.arange(_E)), rep(np.arange(32) * P), rep(np.tril(np.ones((_E, _E)))),
        rep(np.arange(routed)), rep(np.arange(_E) * region), rep([-0.5])], axis=1).astype(f32)
    import ml_dtypes
    consts_b = np.concatenate([s < t, np.ones((P, P))], axis=1).astype(ml_dtypes.bfloat16)
    n = np.arange(tiles)
    token_ids = ((n % 2) * _T + (n // 2) * P)[None, :] + np.arange(P)[:, None]
    token_ids = np.concatenate([token_ids, tokens + np.arange(P)[:, None]], axis=1).astype(np.uint32)

    def chunked(w):
        e, o, i = w.shape
        return np.ascontiguousarray(w.transpose(2, 0, 1).reshape(i // P, P, e, o).transpose(1, 2, 0, 3).reshape(P, e, -1))

    arrays = {
        "x": arr("L0_attn_x").reshape(tokens, _D),
        "w_qk": np.ascontiguousarray(np.concatenate([arr("L0_attn_Wq").T, arr("L0_attn_Wk").T], axis=1)),
        "w_v": np.ascontiguousarray(arr("L0_attn_Wv").T),
        "w_o": np.ascontiguousarray(arr("L0_attn_Wo").T),
        "rope": np.concatenate([cos, cos, -sin, sin], axis=1).astype(f32),
        "norm_scale": arr("L0_ffn_norm_scale").reshape(1, _D),
        "w_router": np.ascontiguousarray(arr("L0_ffn_w_router").T),
        "w_up": chunked(arr("L0_ffn_w_up")),
        "w_down": chunked(arr("L0_ffn_w_down")),
        "consts_f": consts_f,
        "consts_b": consts_b,
        "token_ids": token_ids,
    }
    nc = bacc.Bacc("TRN2", target_bir_lowering=False, num_devices=1)
    aps = [nc.dram_tensor(k, a.shape, mybir.dt.from_np(a.dtype), kind="ExternalInput").ap() for k, a in arrays.items()]
    routed_rows = nc.dram_tensor("routed_rows", [_E * region + P, ROW], F32, kind="Internal").ap()
    out = nc.dram_tensor("out", [tokens + P, _D], F32, kind="ExternalOutput").ap()
    block_kernel(nc, *aps, routed_rows, out, _B, _T, _E, _H)
    r = run_bass_kernel_spmd(nc, [arrays], core_ids=[0])
    return np.asarray(r.results[0]["out"])[0:tokens].reshape(_B, _T, _D)
```

```python
from contextlib import ExitStack

import concourse.bass as bass
from concourse import mybir

P = 128
ALU = mybir.AluOpType
ACT = mybir.ActivationFunctionType
F32 = mybir.dt.float32
BF16 = mybir.dt.bfloat16
U32 = mybir.dt.uint32
AX_X = mybir.AxisListType.X

LN_EPS, RMS_EPS, DEN_EPS = 1e-5, 1e-6, 1e-6
HEAD_DIM = 16
ROW = 260
TOKEN, W_SECOND, W_GAP, FIRST_EXPERT = 256, 257, 258, 259
RING = 4


def sizes(batches, length, dim, experts, hidden):
    tokens = batches * length
    tiles = tokens // P
    region = tokens + P
    routed = (2 * tokens + experts * (P - 1)) // P
    return tokens, tiles, region, routed


class Steps:

    def __init__(self, eng, sem, n, per_tile):
        self.eng, self.sem, self.base, self.per_tile, self.count = eng, sem, n * per_tile, per_tile, 0

    def done(self, ins):
        self.count += 1
        ins.then_inc(self.sem, 1)
        self.eng.wait_ge(self.sem, self.base + self.count)

    def close(self):
        assert self.count == self.per_tile, self.count


def block_kernel(nc, x, w_qk, w_v, w_o, rope, norm_scale, w_router, w_up, w_down, consts_f, consts_b,
                 token_ids, routed_rows, out, batches, length, experts, hidden):
    dim = x.shape[1]
    tokens, tiles, region, routed_tiles = sizes(batches, length, dim, experts, hidden)
    per_batch = tiles // batches
    heads = dim // HEAD_DIM
    KC = dim // P
    HC = hidden // P
    pad_region = experts * region
    assert batches == 2 and KC == 2 and heads == 16 and tiles % RING == 0 and HC == 4
    assert experts == 8 and hidden == 512

    x_out = out[0:tokens, :]

    with ExitStack() as ctx:
        def sb(name, shape, dt=F32):
            return ctx.enter_context(nc.sbuf_tensor(name, shape, dt))

        def psum(name, shape):
            return ctx.enter_context(nc.psum_tensor(name, shape, F32))

        def sem(name):
            return ctx.enter_context(nc.semaphore(name))

        wqk_sb = sb("wqk_sb", [P, KC, 2 * dim])
        wv_sb = sb("wv_sb", [P, KC, dim])
        wo_sb = sb("wo_sb", [P, KC, dim])
        wr_sb = sb("wr_sb", [P, KC, experts])
        rope_sb = sb("rope_sb", [P, per_batch, 2 * HEAD_DIM])
        scale_sb = sb("scale_sb", [P, dim])
        up_sb = sb("up_sb", [P, experts, KC * 2 * hidden])
        down_sb = sb("down_sb", [P, experts, HC * dim])
        NF = consts_f.shape[1]
        cf = sb("cf", [P, NF])
        ident = cf[:, 0:P]
        causal = cf[:, P:2 * P]
        ones = cf[:, 2 * P:3 * P]
        same_head = cf[:, 3 * P:4 * P]
        at = 4 * P
        head_mask = cf[:, at:at + 8]
        at += 8
        expert_iota = cf[:, at:at + experts]
        at += experts
        tile_starts = cf[:, at:at + 32]
        at += 32
        low_tri = cf[:, at:at + experts * experts]
        at += experts * experts
        tile_iota = cf[:, at:at + routed_tiles]
        at += routed_tiles
        region_start = cf[:, at:at + experts]
        at += experts
        minus_half = cf[:, at:at + 1]
        at += 1
        assert at == NF
        cb = sb("cb", [P, 2 * P], BF16)
        earlier = cb[:, 0:P]
        ones_b = cb[:, P:2 * P]
        ids = sb("ids", [P, tiles + 1], U32)

        xin = sb("xin", [P, RING, dim])
        stats1 = sb("stats1", [P, 2, 6])
        mv1 = sb("mv1", [P, 2, 2])
        rstd1 = sb("rstd1", [P, 2, 1])
        xhat = sb("xhat", [P, 2, dim])
        xhatT = sb("xhatT", [P, 2, KC, P])
        rot_a = sb("rot_a", [P, 2 * dim])
        rot_b = sb("rot_b", [P, 2 * dim])
        rot = sb("rot", [P, 2 * dim])
        erot = sb("erot", [P, 2 * dim])
        rot1 = sb("rot1", [P, 2 * dim])
        phi = sb("phi", [P, 2, 2 * dim])
        v_pad = sb("v_pad", [P, 2, heads, 2 * HEAD_DIM])
        kacc = sb("kacc", [P, 2, dim])
        qk_prod = sb("qk_prod", [P, dim])
        den = sb("den", [P, heads])
        rden = sb("rden", [P, heads])
        qn = sb("qn", [P, dim])
        kT = sb("kT", [P, KC, P])
        qT = sb("qT", [P, KC, P])
        q_head = sb("q_head", [P, 8, KC, P])
        attn = sb("attn", [P, 4, 4, P])
        state = sb("state", [P, 2, KC, P])
        state_add = sb("state_add", [P, KC, P])
        yT = sb("yT", [P, KC, P])
        x1 = sb("x1", [P, dim])
        stats2 = sb("stats2", [P, 6])
        mv2 = sb("mv2", [P, 2])
        rstd2 = sb("rstd2", [P, 1])
        ms2 = sb("ms2", [P, 1])
        var1 = sb("var1", [P, 1])
        var2 = sb("var2", [P, 1])
        rms2 = sb("rms2", [P, 1])
        xhat2 = sb("xhat2", [P, dim])
        acc = sb("acc", [P, RING, dim])
        rows = sb("rows", [P, RING, ROW])
        xnT = sb("xnT", [P, KC, P])
        scores8 = sb("scores8", [P, experts])
        top8 = sb("top8", [P, 8])
        top8_at = sb("top8_at", [P, 2, 8], U32)
        onehot = sb("onehot", [P, 2, 2, experts])
        gap = sb("gap", [P, 1])
        egap = sb("egap", [P, 1])
        gap1 = sb("gap1", [P, 1])
        w_first = sb("w_first", [P, 1])
        members = sb("members", [P, 2, experts], BF16)
        macc = sb("macc", [P, experts], BF16)
        rank_prod = sb("rank_prod", [P, 2, experts])
        rank = sb("rank", [P, 2])
        slot_of = sb("slot_of", [P, 2, 2], U32)

        cmp_c = sb("cmp_c", [P, experts, 32])
        counts = sb("counts", [P, experts])
        ntiles = sb("ntiles", [P, experts])
        cum_prod = sb("cum_prod", [P, experts, experts])
        cum = sb("cum", [P, experts])
        past = sb("past", [P, routed_tiles, experts])
        past_n = sb("past_n", [P, routed_tiles, experts])
        expert_f = sb("expert_f", [P, routed_tiles])
        first_f = sb("first_f", [P, routed_tiles])
        start_f = sb("start_f", [P, routed_tiles])
        expert_u = sb("expert_u", [P, routed_tiles], U32)
        start_u = sb("start_u", [P, routed_tiles], U32)
        pad_u = sb("pad_u", [P, experts], U32)
        pad_rows = sb("pad_rows", [P, ROW])

        xr = sb("xr", [P, RING, ROW])
        xrT = sb("xrT", [P, 2, KC, P])
        sgate = sb("sgate", [P, hidden])
        hid = sb("hid", [P, 2, hidden])
        hidT = sb("hidT", [P, HC, P])
        is_first = sb("is_first", [P, 1])
        w_row = sb("w_row", [P, 1])
        y = sb("y", [P, 2, dim])

        bank = [psum(f"bank{k}", [P, 512]) for k in range(8)]
        ps_scores = bank[0:4]
        ps_num, ps_state = bank[0], bank[1]
        ps_qk, ps_xv, ps_qT, ps_small = bank[4], bank[5], bank[6], bank[7]

        weights_in = sem("weights_in")
        experts_in = sem("experts_in")
        x_loaded = [sem(f"x_loaded{u}") for u in range(RING)]
        acc_stored = [sem(f"acc_stored{u}") for u in range(RING)]
        scattered = [sem(f"scattered{u}") for u in range(RING)]
        pads_stored = sem("pads_stored")
        spare_zeroed = sem("spare_zeroed")
        init_done = sem("init_done")
        stats1_ready = sem("stats1_ready")
        mv1_ready = sem("mv1_ready")
        rstd1_ready = sem("rstd1_ready")
        xhat_ready = sem("xhat_ready")
        xhatT_psum = sem("xhatT_psum")
        xhatT_ready = sem("xhatT_ready")
        qk_psum = sem("qk_psum")
        v_psum = sem("v_psum")
        v_ready = sem("v_ready")
        rot_parts_ready = sem("rot_parts_ready")
        rot_ready = sem("rot_ready")
        exp_ready = sem("exp_ready")
        phi_ready = sem("phi_ready")
        kcum_psum = sem("kcum_psum")
        kT_psum = sem("kT_psum")
        kT_ready = sem("kT_ready")
        kacc_ready = sem("kacc_ready")
        kcum_read = sem("kcum_read")
        den_step = sem("den_step")
        rden_ready = sem("rden_ready")
        qn_ready = sem("qn_ready")
        qT_psum = sem("qT_psum")
        q_head_ready = sem("q_head_ready")
        qT_ready = sem("qT_ready")
        scores_psum = sem("scores_psum")
        attn_dve = sem("attn_dve")
        attn_copied = sem("attn_copied")
        attn_pool = sem("attn_pool")
        num_psum = sem("num_psum")
        yT_ready = sem("yT_ready")
        state_psum = sem("state_psum")
        state_add_ready = sem("state_add_ready")
        state_ready = sem("state_ready")
        wo_psum = sem("wo_psum")
        x1_ready = sem("x1_ready")
        stats2_ready = sem("stats2_ready")
        mv2_ready = sem("mv2_ready")
        pool_ln1_step = sem("pool_ln1_step")
        pool_ln2_step = sem("pool_ln2_step")
        rms2_ready = sem("rms2_ready")
        xhat2_ready = sem("xhat2_ready")
        xn_ready = sem("xn_ready")
        acc_ready = sem("acc_ready")
        tok_ready = sem("tok_ready")
        xnT_psum = sem("xnT_psum")
        xnT_ready = sem("xnT_ready")
        logits_psum = sem("logits_psum")
        ranks_psum = sem("ranks_psum")
        route_step = sem("route_step")
        members_ready = sem("members_ready")
        gap_ready = sem("gap_ready")
        egap_ready = sem("egap_ready")
        meta_ready = sem("meta_ready")
        macc_ready = sem("macc_ready")
        rank_step = sem("rank_step")
        slots_ready = sem("slots_ready")
        counts_psum = sem("counts_psum")
        table_step = sem("table_step")
        table_ready = sem("table_ready")
        rows_loaded = [sem(f"rows_loaded{u}") for u in range(RING)]
        xrT_psum = sem("xrT_psum")
        xrT_ready = sem("xrT_ready")
        gate_psum = sem("gate_psum")
        up_psum = sem("up_psum")
        sgate_ready = sem("sgate_ready")
        hid_ready = sem("hid_ready")
        hidT_psum = sem("hidT_psum")
        hidT_ready = sem("hidT_ready")
        down_psum = sem("down_psum")
        w_step = sem("w_step")
        y_ready = sem("y_ready")
        added = sem("added")

        block = ctx.enter_context(nc.Block())

        def alive(n):
            return not isinstance(n, int) or 0 <= n < tiles

        def over_tiles(eng, step):
            for n in range(-3, 2 * RING):
                step(n, n % RING)
            with eng.Fori(2, tiles // RING - 1) as group:
                for u in range(RING):
                    step(group * RING + u, u)
            for n in range(tiles - RING, tiles + 4):
                step(n, n % RING)

        ps_gate, ps_up = [bank[0], bank[1]], [bank[2], bank[3]]
        ps_xrT, ps_hidT, ps_down = bank[4], bank[5], [bank[6], bank[7]]

        def alive2(t):
            return not isinstance(t, int) or 0 <= t < routed_tiles

        def over_routed(eng, step):
            whole = routed_tiles // RING
            for t in range(-1, RING):
                step(t, t % RING)
            with eng.Fori(1, whole) as group:
                for u in range(RING):
                    step(group * RING + u, u)
            for t in range(whole * RING, routed_tiles + 1):
                step(t, t % RING)

        def settle(eng):
            eng.nop(nofuse=True)

        def first_round(n):
            return isinstance(n, int) and n < RING

        def later(n, k=1):
            return not isinstance(n, int) or n >= k

        @block.sync
        def _(sp):
            def x_rows(n, u):
                return bass.ds((u % 2) * length + (n // 2 if isinstance(n, int) else n_half(n, u)) * P, P)

            def n_half(n, u):
                return (n - (u % 2)) // 2

            def load_x(n, u):
                sp.dma_start(xin[:, u, :], x[x_rows(n, u), :]).then_inc(x_loaded[u], 16)

            for n in range(RING):
                load_x(n, n)
            sp.dma_start(cf[:, :], consts_f).then_inc(weights_in, 16)
            sp.dma_start(wqk_sb[:, :, :], w_qk.rearrange("(c p) n -> p c n", p=P)).then_inc(weights_in, 16)
            sp.dma_start(rope_sb[:, :, :], rope.rearrange("(i p) n -> p i n", p=P)).then_inc(weights_in, 16)
            sp.dma_start(ids[:, :], token_ids).then_inc(weights_in, 16)

            def step(n, u):
                m, um = n - 1, (u + 3) % RING
                if alive(m):
                    if not isinstance(m, int) or m + RING < tiles:
                        sp.wait_ge(x1_ready, m + 1)
                        load_x(m + RING, um)
                    sp.wait_ge(acc_ready, m + 1)
                    sp.dma_start(x_out[x_rows(m, um), :], acc[:, um, :]).then_inc(acc_stored[um], 16)

            over_tiles(sp, step)

            sp.wait_ge(table_ready, 1)
            for e in range(experts):
                at_row = sp.value_load(pad_u[0:1, e:e + 1], min_val=0, max_val=pad_region - P)
                sp.dma_start(routed_rows[bass.ds(at_row, P), :], pad_rows[:, :]).then_inc(pads_stored, 16)
            sp.dma_start(routed_rows[pad_region:pad_region + P, :], pad_rows[:, :]).then_inc(pads_stored, 16)
            sp.wait_ge(pads_stored, 16 * (experts + 1))
            for u in range(RING):
                sp.wait_ge(scattered[u], 32 * (tiles // RING))

            def load_rows(t, u):
                if not (isinstance(t, int) and t < RING):
                    sp.wait_ge(added, 16 * (t - RING + 1))
                start = sp.value_load(start_u[0:1, t:t + 1] if isinstance(t, int) else start_u[0:1, bass.ds(t, 1)],
                                      min_val=0, max_val=pad_region)
                sp.dma_start(xr[:, u, :], routed_rows[bass.ds(start, P), :]).then_inc(rows_loaded[u], 16)

            whole = routed_tiles // RING
            for t in range(RING):
                load_rows(t, t)
            with sp.Fori(1, whole) as group:
                for u in range(RING):
                    load_rows(group * RING + u, u)
            for t in range(whole * RING, routed_tiles):
                load_rows(t, t % RING)

        @block.scalar
        def _(act):
            act.dma_start(wv_sb[:, :, :], w_v.rearrange("(c p) n -> p c n", p=P)).then_inc(weights_in, 16)
            act.dma_start(wo_sb[:, :, :], w_o.rearrange("(c p) n -> p c n", p=P)).then_inc(weights_in, 16)
            act.dma_start(wr_sb[:, :, :], w_router.rearrange("(c p) n -> p c n", p=P)).then_inc(weights_in, 16)
            act.dma_start(cb[:, :], consts_b).then_inc(weights_in, 16)
            act.dma_start(scale_sb[:, :], norm_scale.to_broadcast([P, dim])).then_inc(weights_in, 16)
            for e in range(experts):
                act.dma_start(up_sb[:, e, :], w_up[:, e, :]).then_inc(experts_in, 16)
                act.dma_start(down_sb[:, e, :], w_down[:, e, :]).then_inc(experts_in, 16)
            act.wait_ge(weights_in, 16 * 9)
            act.wait_ge(init_done, 1)

            def step(n, u):
                nb = (u + 1) % 2
                m, x = n + 1, n + 2
                if alive(n):
                    act.wait_ge(qT_psum, n + 1)
                    if later(n):
                        act.wait_ge(num_psum, n)
                    for j in range(8):
                        nc.scalar.activation(q_head[:, j, :, :],
                                             ps_qT[:, 0:dim].rearrange("p (c t) -> p c t", c=KC),
                                             ACT.Copy, scale=head_mask[:, j:j + 1]).then_inc(q_head_ready, 1)
                    nc.scalar.activation(qT[:, :, :], ps_qT[:, 0:dim], ACT.Copy).then_inc(qT_ready, 1)
                if alive(m):
                    act.wait_ge(v_psum, m + 1)
                    if later(m, 2):
                        act.wait_ge(state_psum, m - 1)
                    nc.scalar.activation(
                        v_pad[:, nb, :, :].rearrange("p (a b) (c d) -> p a (b c) d", b=2, c=2)[:, :, 0:4:3, :],
                        ps_xv[:, dim:2 * dim], ACT.Copy).then_inc(v_ready, 1)
                if alive(n - 3):
                    act.wait_ge(gap_ready, n - 2)
                    if later(n - 3):
                        act.wait_ge(meta_ready, 3 * (n - 3))
                    nc.scalar.activation(egap[:, :], gap[:, :], ACT.Exp).then_inc(egap_ready, 1)
                    act.wait_ge(egap_ready, 2 * (n - 3) + 1)
                    nc.scalar.activation(gap1[:, :], egap[:, :], ACT.Copy, bias=1.0).then_inc(egap_ready, 1)
                if alive(n):
                    act.wait_ge(scores_psum, 4 * n + 2)
                    nc.scalar.activation(attn[:, 1, :, :], ps_scores[1][:, :], ACT.Copy).then_inc(attn_copied, 1)
                if alive(m):
                    act.wait_ge(rot_ready, m + 1)
                    if later(m):
                        act.wait_ge(phi_ready, m)
                    nc.scalar.activation(erot[:, :], rot[:, :], ACT.Exp).then_inc(exp_ready, 1)
                    nc.scalar.activation(rot1[:, :], rot[:, :], ACT.Copy, bias=1.0).then_inc(exp_ready, 1)
                if alive(n - 2):
                    act.wait_ge(xnT_psum, n - 1)
                    if later(n - 2):
                        act.wait_ge(logits_psum, n - 2)
                    nc.scalar.activation(xnT[:, :, :], ps_xv[:, 0:dim], ACT.Copy).then_inc(xnT_ready, 1)
                if alive(n):
                    act.wait_ge(num_psum, n + 1)
                    if later(n):
                        act.wait_ge(wo_psum, n)
                    nc.scalar.activation(yT[:, :, :], ps_num[:, 0:dim], ACT.Copy).then_inc(yT_ready, 1)
                if alive(x):
                    act.wait_ge(xhatT_psum, x + 1)
                    if later(x, 2):
                        act.wait_ge(v_psum, x - 1)
                    nc.scalar.activation(xhatT[:, u % 2, :, :], ps_qT[:, dim:2 * dim], ACT.Copy).then_inc(xhatT_ready, 1)
                if alive(m):
                    act.wait_ge(kT_psum, m + 1)
                    nc.scalar.activation(kT[:, :, :], ps_xv[:, dim:2 * dim], ACT.Copy).then_inc(kT_ready, 1)

            over_tiles(act, step)

            def gate(t):
                act.wait_ge(gate_psum, t + 1)
                if not (isinstance(t, int) and t < 1):
                    act.wait_ge(hid_ready, t)
                return act

            def step2(t, u):
                b = u % 2
                if alive2(t + 1):
                    act.wait_ge(xrT_psum, t + 2)
                    nc.scalar.activation(xrT[:, 1 - b, :, :], ps_xrT[:, 0:dim], ACT.Copy).then_inc(xrT_ready, 1)
                if alive2(t - 1):
                    act.wait_ge(hidT_psum, t)
                    nc.scalar.activation(hidT[:, :, :], ps_hidT[:, :], ACT.Copy).then_inc(hidT_ready, 1)
                if alive2(t):
                    gate(t)
                    nc.scalar.activation(sgate[:, :], ps_gate[b][:, :], ACT.Silu).then_inc(sgate_ready, 1)

            over_routed(act, step2)

        @block.vector
        def _(dve):
            nc.vector.memset(v_pad[:, :, :, :], 0.0).then_inc(init_done, 1)
            nc.vector.memset(pad_rows[:, :], 0.0).then_inc(table_step, 1)
            dve.wait_ge(weights_in, 16 * 9)
            dve.wait_ge(table_step, 1)
            nc.vector.tensor_copy(pad_rows[:, TOKEN:TOKEN + 1].bitcast(U32), ids[:, tiles:tiles + 1]).then_inc(table_step, 1)

            def stats_first(n, u):
                dve.wait_ge(x_loaded[u], 4 * (n - u) + 16)
                if later(n, 2):
                    dve.wait_ge(mv1_ready, n - 1)
                nc.vector.bn_stats(stats1[:, u % 2, :], xin[:, u, :]).then_inc(stats1_ready, 1)

            def moments_first(n, u):
                b = u % 2
                dve.wait_ge(stats1_ready, n + 1)
                if later(n, 2):
                    dve.wait_ge(rstd1_ready, n - 1)
                settle(dve)
                nc.vector.bn_aggr(mv1[:, b, :], stats1[:, b, :]).then_inc(mv1_ready, 1)

            def norm1(n, u):
                b = u % 2
                dve.wait_ge(rstd1_ready, n + 1)
                dve.wait_ge(mv1_ready, n + 1)
                if later(n, 2):
                    dve.wait_ge(xhatT_psum, n - 1)
                nc.vector.tensor_scalar(xhat[:, b, :], xin[:, u, :], mv1[:, b, 0:1], rstd1[:, b, :],
                                        ALU.subtract, ALU.mult).then_inc(xhat_ready, 1)

            def mask(n, g):
                if later(n):
                    dve.wait_ge(num_psum, n)
                dve.wait_ge(scores_psum, 4 * n + g + 1)
                nc.vector.tensor_tensor(attn[:, g, :, :], ps_scores[g][:, :].rearrange("p (h t) -> p h t", h=4),
                                        causal.unsqueeze(1).to_broadcast([P, 4, P]), ALU.mult).then_inc(attn_dve, 1)

            half = HEAD_DIM // 2

            def rope_table(n, u):
                i = n // 2 if isinstance(n, int) else (n - u % 2) // 2
                return rope_sb[:, bass.ds(i, 1), :].rearrange("p i n -> p (i n)")

            def rotate_cos(n, u):
                cos = rope_table(n, u)[:, 0:HEAD_DIM].unsqueeze(1).to_broadcast([P, 2 * heads, HEAD_DIM])
                dve.wait_ge(qk_psum, n + 1)
                if later(n):
                    dve.wait_ge(rot_ready, n)
                nc.vector.tensor_tensor(rot_a[:, :].rearrange("p (h d) -> p h d", d=HEAD_DIM),
                                        ps_qk[:, :].rearrange("p (h d) -> p h d", d=HEAD_DIM), cos,
                                        ALU.mult).then_inc(rot_parts_ready, 1)

            def rotate_sin(n, u, k):
                sin = rope_table(n, u)[:, HEAD_DIM + k * half:HEAD_DIM + (k + 1) * half].unsqueeze(1)
                qk = ps_qk[:, :].rearrange("p (h d) -> p h d", d=HEAD_DIM)
                nc.vector.tensor_tensor(rot_b[:, :].rearrange("p (h d) -> p h d", d=HEAD_DIM)[:, :, k * half:(k + 1) * half],
                                        qk[:, :, (1 - k) * half:(2 - k) * half],
                                        sin.to_broadcast([P, 2 * heads, half]), ALU.mult).then_inc(rot_parts_ready, 1)

            def features(n, u):
                dve.wait_ge(exp_ready, 2 * n + 2)
                if later(n, 2):
                    dve.wait_ge(state_psum, n - 1)
                nc.vector.scalar_tensor_tensor(phi[:, u % 2, :], erot[:, :], 1.0, rot1[:, :], ALU.min,
                                               ALU.max).then_inc(phi_ready, 1)

            def state_part(n, u):
                dve.wait_ge(state_psum, n + 1)
                if later(n):
                    dve.wait_ge(state_ready, n)
                nc.vector.tensor_tensor(state_add[:, :, :],
                                        ps_state[:, 0:dim].rearrange("p (c t) -> p c t", c=KC),
                                        same_head.unsqueeze(1).to_broadcast([P, KC, P]),
                                        ALU.mult).then_inc(state_add_ready, 1)

            def key_products(n, u):
                dve.wait_ge(kcum_psum, n + 1)
                dve.wait_ge(phi_ready, n + 1)
                nc.vector.tensor_tensor(qk_prod[:, :], ps_small[:, 0:dim], phi[:, u % 2, 0:dim],
                                        ALU.mult).then_inc(kcum_read, 1)

            def key_sums(n):
                dve.wait_ge(kcum_read, n + 1)
                nc.vector.tensor_reduce(den[:, :], qk_prod[:, :].rearrange("p (h d) -> p h d", d=HEAD_DIM),
                                        AX_X, ALU.add).then_inc(den_step, 1)

            def denominators(n):
                dve.wait_ge(den_step, 2 * n + 1)
                nc.vector.tensor_scalar(den[:, :], den[:, :], DEN_EPS, None, ALU.max).then_inc(den_step, 1)
                dve.wait_ge(den_step, 2 * n + 2)
                if later(n):
                    dve.wait_ge(qn_ready, n)
                nc.vector.reciprocal(rden[:, :], den[:, :]).then_inc(rden_ready, 1)

            def residual(n, u):
                dve.wait_ge(wo_psum, n + 1)
                if later(n):
                    dve.wait_ge(acc_ready, n)
                    dve.wait_ge(xhat2_ready, n)
                nc.vector.tensor_tensor(x1[:, :], ps_small[:, 0:dim], xin[:, u, :], ALU.add).then_inc(x1_ready, 1)

            def stats_second(n):
                dve.wait_ge(x1_ready, n + 1)
                nc.vector.bn_stats(stats2[:, :], x1[:, :]).then_inc(stats2_ready, 1)

            def moments_second(n):
                dve.wait_ge(stats2_ready, n + 1)
                if later(n):
                    dve.wait_ge(rms2_ready, n)
                settle(dve)
                nc.vector.bn_aggr(mv2[:, :], stats2[:, :]).then_inc(mv2_ready, 1)

            def norm2(n):
                dve.wait_ge(rms2_ready, n + 1)
                dve.wait_ge(mv2_ready, n + 1)
                nc.vector.tensor_scalar(xhat2[:, :], x1[:, :], mv2[:, 0:1], rstd2[:, :],
                                        ALU.subtract, ALU.mult).then_inc(xhat2_ready, 1)

            def expert_input(n, u):
                dve.wait_ge(xhat2_ready, n + 1)
                if not first_round(n):
                    dve.wait_ge(scattered[u], 8 * (n - u))
                nc.vector.scalar_tensor_tensor(rows[:, u, 0:dim], xhat2[:, :], rms2[:, :], scale_sb[:, :],
                                               ALU.mult, ALU.mult).then_inc(xn_ready, 1)

            def copy_logits(n):
                dve.wait_ge(logits_psum, n + 1)
                nc.vector.tensor_copy(scores8[:, :], ps_small[:, 256:256 + experts]).then_inc(route_step, 1)

            def top_values(n):
                dve.wait_ge(route_step, 5 * n + 1)
                settle(dve)
                nc.vector.max(top8[:, :], scores8[:, :]).then_inc(route_step, 1)

            def top_gap(n):
                dve.wait_ge(route_step, 5 * n + 2)
                if later(n):
                    dve.wait_ge(egap_ready, 2 * n)
                nc.vector.tensor_tensor(gap[:, :], top8[:, 1:2], top8[:, 0:1], ALU.subtract).then_inc(gap_ready, 1)

            def top_experts(n, u):
                nc.vector.max_index(top8_at[:, u % 2, :], top8[:, :], scores8[:, :]).then_inc(route_step, 1)

            def one_hots(n, u):
                b = u % 2
                dve.wait_ge(route_step, 5 * n + 3)
                nc.vector.tensor_tensor(
                    onehot[:, b, :, :], expert_iota.unsqueeze(1).to_broadcast([P, 2, experts]),
                    top8_at[:, b, 0:2].unsqueeze(2).to_broadcast([P, 2, experts]), ALU.is_equal).then_inc(route_step, 1)

            def member_rows(n, u):
                b = u % 2
                dve.wait_ge(route_step, 5 * n + 4)
                if later(n, 2):
                    dve.wait_ge(macc_ready, n - 1)
                nc.vector.tensor_tensor(members[:, b, :], onehot[:, b, 0, :], onehot[:, b, 1, :],
                                        ALU.add).then_inc(members_ready, 1)

            def first_weight(n):
                dve.wait_ge(egap_ready, 2 * n + 2)
                nc.vector.reciprocal(w_first[:, :], gap1[:, :]).then_inc(route_step, 1)

            def second_weight(n, u):
                dve.wait_ge(route_step, 5 * n + 5)
                nc.vector.tensor_tensor(rows[:, u, W_SECOND:W_SECOND + 1], w_first[:, :], egap[:, :],
                                        ALU.mult).then_inc(meta_ready, 1)

            def weight_gap(n, u):
                dve.wait_ge(meta_ready, 3 * n + 1)
                nc.vector.tensor_tensor(rows[:, u, W_GAP:W_GAP + 1], w_first[:, :],
                                        rows[:, u, W_SECOND:W_SECOND + 1], ALU.subtract).then_inc(meta_ready, 1)
                nc.vector.tensor_copy(rows[:, u, FIRST_EXPERT:FIRST_EXPERT + 1],
                                      top8_at[:, u % 2, 0:1]).then_inc(meta_ready, 1)

            def rank_products(n, u):
                dve.wait_ge(ranks_psum, n + 1)
                nc.vector.tensor_tensor(
                    rank_prod[:, :, :], ps_small[:, 264:264 + experts].unsqueeze(1).to_broadcast([P, 2, experts]),
                    onehot[:, u % 2, :, :], ALU.mult).then_inc(rank_step, 1)

            def rank_sums(n):
                dve.wait_ge(rank_step, 2 * n + 1)
                nc.vector.tensor_reduce(rank[:, :], rank_prod[:, :, :], AX_X, ALU.add).then_inc(rank_step, 1)

            def places(n, u):
                b, before = u % 2, (u + 2) % RING
                dve.wait_ge(rank_step, 2 * n + 2)
                if later(n, 2):
                    dve.wait_ge(scattered[before], 8 * (n - 2 - before) + 32)
                nc.vector.scalar_tensor_tensor(slot_of[:, b, :], top8_at[:, b, 0:2], float(region), rank[:, :],
                                               ALU.mult, ALU.add).then_inc(slots_ready, 1)

            def step(n, u):
                m, a, r = n + 1, n - 1, n - 3
                um, ua, ur = (u + 1) % RING, (u + 3) % RING, (u + 1) % RING
                if alive(m):
                    rotate_cos(m, um)
                if alive(r):
                    copy_logits(r)
                if alive(m):
                    rotate_sin(m, um, 0)
                if alive(r):
                    top_values(r)
                if alive(m):
                    rotate_sin(m, um, 1)
                if alive(r):
                    top_gap(r)
                    top_experts(r, ur)
                if alive(a):
                    residual(a, ua)
                if alive(r):
                    one_hots(r, ur)
                if alive(a):
                    stats_second(a)
                if alive(r):
                    member_rows(r, ur)
                if alive(n):
                    mask(n, 0)
                if alive(a):
                    moments_second(a)
                if alive(n + 2):
                    norm1(n + 2, (u + 2) % RING)
                if alive(n):
                    mask(n, 2)
                    mask(n, 3)
                if alive(r):
                    first_weight(r)
                if alive(m):
                    features(m, um)
                if alive(r):
                    second_weight(r, ur)
                if alive(a):
                    norm2(a)
                if alive(r):
                    weight_gap(r, ur)
                if alive(a):
                    expert_input(a, ua)
                if alive(n):
                    state_part(n, u)
                if alive(r):
                    rank_products(r, ur)
                if alive(n + 3):
                    stats_first(n + 3, (u + 3) % RING)
                if alive(r):
                    rank_sums(r)
                if alive(m):
                    key_products(m, um)
                if alive(r):
                    places(r, ur)
                if alive(m):
                    key_sums(m)
                if alive(n + 3):
                    moments_first(n + 3, (u + 3) % RING)
                if alive(m):
                    denominators(m)

            over_tiles(dve, step)

            done = [2]

            def link(ins):
                done[0] += 1
                ins.then_inc(table_step, 1)
                dve.wait_ge(table_step, done[0])

            NT = routed_tiles
            dve.wait_ge(counts_psum, 1)
            link(nc.vector.tensor_copy(counts[:, :], ps_small[:, 272:272 + experts]))
            link(nc.vector.tensor_tensor(cmp_c[:, :, :], counts[:, :].unsqueeze(2).to_broadcast([P, experts, 32]),
                                         tile_starts.unsqueeze(1).to_broadcast([P, experts, 32]), ALU.is_gt))
            link(nc.vector.tensor_reduce(ntiles[:, :], cmp_c[:, :, :], AX_X, ALU.add))
            link(nc.vector.tensor_tensor(cum_prod[:, :, :], low_tri.rearrange("p (e f) -> p e f", e=experts),
                                         ntiles[:, :].unsqueeze(1).to_broadcast([P, experts, experts]), ALU.mult))
            link(nc.vector.tensor_reduce(cum[:, :], cum_prod[:, :, :], AX_X, ALU.add))
            link(nc.vector.tensor_tensor(past[:, :, :], tile_iota.unsqueeze(2).to_broadcast([P, NT, experts]),
                                         cum[:, :].unsqueeze(1).to_broadcast([P, NT, experts]), ALU.is_ge))
            link(nc.vector.tensor_reduce(expert_f[:, :], past[:, :, :], AX_X, ALU.add))
            link(nc.vector.tensor_tensor(past_n[:, :, :], past[:, :, :],
                                         ntiles[:, :].unsqueeze(1).to_broadcast([P, NT, experts]), ALU.mult))
            link(nc.vector.tensor_reduce(first_f[:, :], past_n[:, :, :], AX_X, ALU.add))
            link(nc.vector.tensor_tensor(start_f[:, :], tile_iota, first_f[:, :], ALU.subtract))
            link(nc.vector.tensor_scalar(start_f[:, :], start_f[:, :], float(P), None, ALU.mult))
            link(nc.vector.scalar_tensor_tensor(start_f[:, :], expert_f[:, :], float(region), start_f[:, :],
                                                ALU.mult, ALU.add))
            link(nc.vector.tensor_scalar(start_u[:, :], start_f[:, :], float(pad_region), None, ALU.min))
            link(nc.vector.tensor_scalar(expert_f[:, :], expert_f[:, :], float(experts - 1), None, ALU.min))
            link(nc.vector.tensor_copy(expert_u[:, :], expert_f[:, :]))
            nc.vector.tensor_tensor(pad_u[:, :], region_start, counts[:, :], ALU.add).then_inc(table_ready, 1)

            def hidden_product(t, u):
                b = u % 2
                dve.wait_ge(up_psum, t + 1)
                dve.wait_ge(sgate_ready, t + 1)
                if not (isinstance(t, int) and t < 2):
                    dve.wait_ge(hidT_psum, t - 1)
                nc.vector.tensor_tensor(hid[:, b, :], ps_up[b][:, :], sgate[:, :], ALU.mult).then_inc(hid_ready, 1)

            def weigh(t, u):
                b = u % 2
                s = Steps(dve, w_step, t, 2)
                dve.wait_ge(rows_loaded[u], 4 * (t - u) + 16)
                e_t = expert_f[:, t:t + 1] if isinstance(t, int) else expert_f[:, bass.ds(t, 1)]
                s.done(nc.vector.tensor_tensor(is_first[:, :], xr[:, u, FIRST_EXPERT:FIRST_EXPERT + 1], e_t, ALU.is_equal))
                s.done(nc.vector.scalar_tensor_tensor(w_row[:, :], is_first[:, :], xr[:, u, W_GAP:W_GAP + 1],
                                                      xr[:, u, W_SECOND:W_SECOND + 1], ALU.mult, ALU.add))
                dve.wait_ge(down_psum, t + 1)
                if not (isinstance(t, int) and t < 2):
                    dve.wait_ge(added, 16 * (t - 1))
                nc.vector.tensor_scalar(y[:, b, :], ps_down[b][:, 0:dim], w_row[:, :], None,
                                        ALU.mult).then_inc(y_ready, 1)
                s.close()

            def step2(t, u):
                if alive2(t):
                    hidden_product(t, u)
                if alive2(t - 1):
                    weigh(t - 1, (u + 3) % RING)

            over_routed(dve, step2)

        @block.gpsimd
        def _(pool):
            nc.gpsimd.memset(state[:, :, :, :], 0.0).then_inc(init_done, 1)
            nc.gpsimd.memset(kacc[:, :, :], 0.0).then_inc(init_done, 1)
            nc.gpsimd.memset(macc[:, :], 0.0).then_inc(init_done, 1)
            pool.wait_ge(init_done, 4)
            pool.wait_ge(weights_in, 16 * 9)
            pool.wait_ge(table_step, 2)
            pool.dma_start(out[tokens:tokens + P, :], pad_rows[:, 0:dim]).then_inc(spare_zeroed, 16)

            def rstd_first(n, u):
                b = u % 2
                pool.wait_ge(mv1_ready, n + 1)
                if later(n, 2):
                    pool.wait_ge(xhat_ready, n - 1)
                s = Steps(pool, pool_ln1_step, n, 1)
                settle(pool)
                s.done(nc.gpsimd.tensor_scalar(var1[:, :], mv1[:, b, 1:2], LN_EPS, None, ALU.add))
                nc.gpsimd.tensor_tensor(rstd1[:, b, :], var1[:, :], minus_half, ALU.pow).then_inc(rstd1_ready, 1)
                s.close()

            def rotated(n, u):
                pool.wait_ge(rot_parts_ready, 3 * n + 3)
                if later(n):
                    pool.wait_ge(exp_ready, 2 * n)
                nc.gpsimd.tensor_tensor(rot[:, :], rot_a[:, :], rot_b[:, :], ALU.add).then_inc(rot_ready, 1)

            def mask(n, u):
                pool.wait_ge(attn_copied, n + 1)
                nc.gpsimd.tensor_tensor(attn[:, 1, :, :], attn[:, 1, :, :],
                                        causal.unsqueeze(1).to_broadcast([P, 4, P]), ALU.mult).then_inc(attn_pool, 1)

            def state_sum(n, u):
                b = u % 2
                pool.wait_ge(state_add_ready, n + 1)
                pool.wait_ge(num_psum, n + 1)
                if later(n, 2):
                    pool.wait_ge(state_ready, n - 1)
                nc.gpsimd.tensor_tensor(state[:, b, :, :], state[:, b, :, :], state_add[:, :, :],
                                        ALU.add).then_inc(state_ready, 1)

            def key_sum(n, u):
                b = u % 2
                pool.wait_ge(kcum_psum, n + 1)
                pool.wait_ge(phi_ready, n + 1)
                if later(n, 2):
                    pool.wait_ge(kacc_ready, n - 1)
                nc.gpsimd.tensor_tensor(kacc[:, b, :], kacc[:, b, :], phi[:, b, dim:2 * dim],
                                        ALU.add).then_inc(kacc_ready, 1)

            def scale_q(n, u):
                b = u % 2
                pool.wait_ge(rden_ready, n + 1)
                if later(n):
                    pool.wait_ge(qT_psum, n)
                nc.gpsimd.tensor_tensor(qn[:, :].rearrange("p (h d) -> p h d", d=HEAD_DIM),
                                        phi[:, b, 0:dim].rearrange("p (h d) -> p h d", d=HEAD_DIM),
                                        rden[:, :].unsqueeze(2).to_broadcast([P, heads, HEAD_DIM]),
                                        ALU.mult).then_inc(qn_ready, 1)

            def norm2_scales(n, u):
                s = Steps(pool, pool_ln2_step, n, 4)
                pool.wait_ge(mv2_ready, n + 1)
                if later(n):
                    pool.wait_ge(xn_ready, n)
                settle(pool)
                s.done(nc.gpsimd.tensor_scalar(var2[:, :], mv2[:, 1:2], LN_EPS, None, ALU.add))
                s.done(nc.gpsimd.tensor_tensor(rstd2[:, :], var2[:, :], minus_half, ALU.pow))
                settle(pool)
                s.done(nc.gpsimd.tensor_scalar(ms2[:, :], rstd2[:, :], rstd2[:, :], mv2[:, 1:2], ALU.mult, ALU.mult))
                settle(pool)
                s.done(nc.gpsimd.tensor_scalar(ms2[:, :], ms2[:, :], RMS_EPS, None, ALU.add))
                nc.gpsimd.tensor_tensor(rms2[:, :], ms2[:, :], minus_half, ALU.pow).then_inc(rms2_ready, 1)
                s.close()

            def accumulate(n, u):
                pool.wait_ge(xhat2_ready, n + 1)
                if not first_round(n):
                    pool.wait_ge(acc_stored[u], 4 * (n - u))
                nc.gpsimd.tensor_tensor(acc[:, u, :], x1[:, :], xhat2[:, :], ALU.add).then_inc(acc_ready, 1)

            def token_column(n, u):
                if not first_round(n):
                    pool.wait_ge(scattered[u], 8 * (n - u))
                nc.gpsimd.tensor_copy(rows[:, u, TOKEN:TOKEN + 1].bitcast(U32),
                                      ids[:, n:n + 1] if isinstance(n, int) else ids[:, bass.ds(n, 1)]).then_inc(tok_ready, 1)

            def member_sum(n, u):
                b = u % 2
                pool.wait_ge(ranks_psum, n + 1)
                pool.wait_ge(members_ready, n + 1)
                if later(n):
                    pool.wait_ge(macc_ready, n)
                nc.gpsimd.tensor_tensor(macc[:, :], macc[:, :], members[:, b, :], ALU.add).then_inc(macc_ready, 1)

            def scatter(n, u):
                b = u % 2
                pool.wait_ge(slots_ready, n + 1)
                pool.wait_ge(meta_ready, 3 * n + 3)
                pool.wait_ge(xn_ready, n + 1)
                pool.wait_ge(tok_ready, n + 1)
                settle(pool)
                for k in range(2):
                    pool.indirect_dma_start(out=routed_rows[:, :],
                                            out_offset=bass.IndirectOffsetOnAxis(ap=slot_of[:, b, k:k + 1], axis=0),
                                            in_=rows[:, u, :], in_offset=None).then_inc(scattered[u], 16)

            def step(n, u):
                m, um, ua, ur = n + 1, (u + 1) % RING, (u + 3) % RING, (u + 1) % RING
                if alive(m):
                    rotated(m, um)
                if alive(n - 4):
                    scatter(n - 4, u)
                if alive(n):
                    mask(n, u)
                if alive(n - 1):
                    norm2_scales(n - 1, ua)
                    token_column(n - 1, ua)
                    accumulate(n - 1, ua)
                if alive(n):
                    state_sum(n, u)
                if alive(m):
                    scale_q(m, um)
                    key_sum(m, um)
                if alive(n + 3):
                    rstd_first(n + 3, (u + 3) % RING)
                if alive(n - 3):
                    member_sum(n - 3, ur)

            over_tiles(pool, step)

            for u in range(RING):
                pool.wait_ge(acc_stored[u], 16 * (tiles // RING))
            pool.wait_ge(spare_zeroed, 16)

            def step2(t, u):
                if not alive2(t - 1):
                    return
                t, u = t - 1, (u + 3) % RING
                pool.wait_ge(y_ready, t + 1)
                if not (isinstance(t, int) and t < 1):
                    pool.wait_ge(added, 16 * t)
                settle(pool)
                pool.indirect_dma_start(
                    out=out[:, :], out_offset=bass.IndirectOffsetOnAxis(ap=xr[:, u, TOKEN:TOKEN + 1].bitcast(U32), axis=0),
                    in_=y[:, u % 2, :], in_offset=None, compute_op=ALU.add).then_inc(added, 16)

            over_routed(pool, step2)
            pool.wait_ge(added, 16 * routed_tiles)

        @block.tensor
        def _(pe):
            pe.wait_ge(weights_in, 16 * 9)
            pe.wait_ge(init_done, 4)

            def transposes(dst, src, chunks):
                for c in range(chunks):
                    last = nc.tensor.transpose(dst[:, c * P:(c + 1) * P], src[:, c * P:(c + 1) * P], ident)
                return last

            def product(dst, lhs, rhs, chunks):
                for c in range(chunks):
                    last = nc.tensor.matmul(dst, lhs(c), rhs(c), start=c == 0, stop=c == chunks - 1)
                return last

            def transpose_x(n, u):
                pe.wait_ge(xhat_ready, n + 1)
                if later(n, 2):
                    pe.wait_ge(qT_ready, n - 1)
                transposes(ps_qT[:, dim:2 * dim], xhat[:, u % 2, :], KC).then_inc(xhatT_psum, 1)

            def scores(n, u):
                pe.wait_ge(kT_ready, n + 1)
                if later(n):
                    pe.wait_ge(yT_ready, n)
                    pe.wait_ge(state_add_ready, n)
                for i in range(2):
                    pe.wait_ge(q_head_ready, 8 * n + 4 * i + 4)
                    for c in range(KC):
                        nc.tensor.matmul(ps_scores[2 * i + c][:, :], kT[:, c, :], q_head[:, 4 * i:4 * i + 4, c, :],
                                         start=True, stop=True).then_inc(scores_psum, 1)

            def project_qk(n, u):
                b = u % 2
                pe.wait_ge(xhatT_ready, n + 1)
                if later(n):
                    pe.wait_ge(rot_parts_ready, 3 * n)
                product(ps_qk[:, :], lambda c: xhatT[:, b, c, :], lambda c: wqk_sb[:, c, :], KC).then_inc(qk_psum, 1)

            def project_v(n, u):
                b = u % 2
                if later(n):
                    pe.wait_ge(kT_ready, n)
                product(ps_xv[:, dim:2 * dim], lambda c: xhatT[:, b, c, :], lambda c: wv_sb[:, c, :], KC).then_inc(v_psum, 1)

            def v_of(b, c):
                v = v_pad[:, b, 8 * c:8 * c + 8, :].rearrange("p (a b) (c d) -> p a (b c) d", b=2, c=2)
                return v[:, :, 0:4:3, :]

            def attend(n, u):
                b = u % 2
                pe.wait_ge(attn_dve, 3 * n + 3)
                pe.wait_ge(attn_pool, n + 1)
                pe.wait_ge(v_ready, n + 1)
                pe.wait_ge(qT_ready, n + 1)
                if later(n, 2):
                    pe.wait_ge(state_ready, n - 1)
                for c in range(KC):
                    nc.tensor.matmul(ps_num[:, c * P:(c + 1) * P], state[:, b, c, :], qT[:, c, :],
                                     start=c == 0, stop=False, skip_group_check=True)
                for c in range(KC):
                    for par in range(2):
                        for g in range(4):
                            last = nc.tensor.matmul(ps_num[32 * g:32 * g + 32, c * P:(c + 1) * P],
                                                    v_pad[:, b, 8 * c + 2 * g + par, :],
                                                    attn[:, 2 * (g // 2) + c, 2 * (g % 2) + par, :],
                                                    start=False, stop=c == KC - 1 and par == 1, skip_group_check=True)
                last.then_inc(num_psum, 1)
                for c in range(KC):
                    last = nc.tensor.matmul(ps_state[:, c * P:(c + 1) * P], phi[:, b, dim + c * P:dim + (c + 1) * P],
                                            v_of(b, c), start=True, stop=True)
                last.then_inc(state_psum, 1)

            def key_prefix(n, u):
                b = u % 2
                pe.wait_ge(phi_ready, n + 1)
                if later(n, 2):
                    pe.wait_ge(kacc_ready, n - 1)
                if later(n, 4):
                    pe.wait_ge(rank_step, 2 * (n - 4) + 1)
                elif later(n, 2):
                    pe.wait_ge(x1_ready, n - 1)
                k = phi[:, b, dim:2 * dim]
                nc.tensor.matmul(ps_small[:, 0:dim], causal, k, start=True, stop=False)
                nc.tensor.matmul(ps_small[:, 0:dim], ones, kacc[:, b, :], start=False, stop=True).then_inc(kcum_psum, 1)
                if later(n, 3):
                    pe.wait_ge(xnT_ready, n - 2)
                transposes(ps_xv[:, dim:2 * dim], k, KC).then_inc(kT_psum, 1)

            def output_projection(n, u):
                pe.wait_ge(yT_ready, n + 1)
                if later(n, 2):
                    pe.wait_ge(route_step, 5 * (n - 2) + 1)
                product(ps_small[:, 0:dim], lambda c: yT[:, c, :], lambda c: wo_sb[:, c, :], KC).then_inc(wo_psum, 1)

            def transpose_xn(n, u):
                pe.wait_ge(xn_ready, n + 1)
                if n + 3 < tiles if isinstance(n, int) else True:
                    pe.wait_ge(v_ready, n + 4)
                transposes(ps_xv, rows[:, u, 0:dim], KC).then_inc(xnT_psum, 1)

            def logits(n, u):
                pe.wait_ge(xnT_ready, n + 1)
                product(ps_small[:, 256:256 + experts], lambda c: xnT[:, c, :], lambda c: wr_sb[:, c, :], KC).then_inc(logits_psum, 1)

            def ranks(n, u):
                pe.wait_ge(members_ready, n + 1)
                if later(n):
                    pe.wait_ge(macc_ready, n)
                if n + 2 < tiles if isinstance(n, int) else True:
                    pe.wait_ge(x1_ready, n + 3)
                else:
                    pe.wait_ge(route_step, 5 * n + 1)
                nc.tensor.matmul(ps_small[:, 264:264 + experts], earlier, members[:, u % 2, :], start=True, stop=False)
                nc.tensor.matmul(ps_small[:, 264:264 + experts], ones_b, macc[:, :], start=False, stop=True).then_inc(ranks_psum, 1)

            def transpose_q(n, u):
                pe.wait_ge(qn_ready, n + 1)
                if later(n):
                    pe.wait_ge(qT_ready, n)
                transposes(ps_qT, qn[:, :], KC).then_inc(qT_psum, 1)

            def step(n, u):
                m, um, ua, uc, ur = n + 1, (u + 1) % RING, (u + 3) % RING, (u + 2) % RING, (u + 1) % RING
                if alive(m):
                    project_qk(m, um)
                if alive(n - 3):
                    if alive(n):
                        pe.wait_ge(kcum_read, n + 1)
                    else:
                        pe.wait_ge(rank_step, 2 * (n - 4) + 1)
                    logits(n - 3, ur)
                if alive(n):
                    transpose_q(n, u)
                if alive(m):
                    project_v(m, um)
                if alive(n - 1):
                    output_projection(n - 1, ua)
                if alive(n):
                    scores(n, u)
                if alive(n - 2):
                    transpose_xn(n - 2, uc)
                if alive(n):
                    attend(n, u)
                if alive(n - 3):
                    ranks(n - 3, ur)
                if alive(n + 2):
                    transpose_x(n + 2, (u + 2) % RING)
                if alive(m):
                    key_prefix(m, um)

            over_tiles(pe, step)

            pe.wait_ge(macc_ready, tiles)
            pe.wait_ge(rank_step, 2 * tiles - 1)
            pe.wait_ge(route_step, 5 * tiles - 4)
            nc.tensor.matmul(ps_small[:, 272:272 + experts], ones_b, macc[:, :], start=True, stop=True).then_inc(counts_psum, 1)

            pe.wait_ge(experts_in, 16 * 2 * experts)
            pe.wait_ge(table_ready, 1)

            def transpose_rows(t, u):
                pe.wait_ge(rows_loaded[u], 4 * (t - u) + 16)
                if not (isinstance(t, int) and t < 1):
                    pe.wait_ge(xrT_ready, t)
                transposes(ps_xrT, xr[:, u, 0:dim], KC).then_inc(xrT_psum, 1)

            def expert_of(t):
                return pe.value_load(expert_u[0:1, t:t + 1] if isinstance(t, int) else expert_u[0:1, bass.ds(t, 1)],
                                     min_val=0, max_val=experts - 1)

            def up(t, u, e):
                b = u % 2
                pe.wait_ge(xrT_ready, t + 1)
                if not (isinstance(t, int) and t < 2):
                    pe.wait_ge(sgate_ready, t - 1)
                    pe.wait_ge(hid_ready, t - 1)
                for half, (dst, signal) in enumerate([(ps_up, up_psum), (ps_gate, gate_psum)][::-1]):
                    at0 = hidden * (1 - half)
                    for c in range(KC):
                        w = up_sb[:, bass.ds(e, 1), c * 2 * hidden + at0:c * 2 * hidden + at0 + hidden]
                        last = nc.tensor.matmul(dst[b][:, :], xrT[:, b, c, :], w.rearrange("p e n -> p (e n)"),
                                                start=c == 0, stop=c == KC - 1)
                    last.then_inc(signal, 1)

            def transpose_hidden(t, u):
                pe.wait_ge(hid_ready, t + 1)
                if not (isinstance(t, int) and t < 1):
                    pe.wait_ge(hidT_ready, t)
                transposes(ps_hidT, hid[:, u % 2, :], HC).then_inc(hidT_psum, 1)

            def down(t, u):
                b = u % 2
                e = expert_of(t)
                pe.wait_ge(hidT_ready, t + 1)
                if not (isinstance(t, int) and t < 2):
                    pe.wait_ge(y_ready, t - 1)
                for c in range(HC):
                    w = down_sb[:, bass.ds(e, 1), c * dim:(c + 1) * dim]
                    last = nc.tensor.matmul(ps_down[b][:, 0:dim], hidT[:, c, :], w.rearrange("p e n -> p (e n)"),
                                            start=c == 0, stop=c == HC - 1)
                last.then_inc(down_psum, 1)

            def step2(t, u):
                e = expert_of(t) if alive2(t) else None
                if alive2(t + 1):
                    transpose_rows(t + 1, (u + 1) % RING)
                if alive2(t - 1):
                    transpose_hidden(t - 1, (u + 3) % RING)
                if alive2(t):
                    up(t, u, e)
                if alive2(t - 1):
                    down(t - 1, (u + 3) % RING)

            over_routed(pe, step2)


_B, _T, _D, _E, _H = 2, 2048, 256, 8, 512


def kernel(**inputs):
    import numpy as np
    import concourse.bacc as bacc
    from concourse.bass_utils import run_bass_kernel_spmd

    f32 = np.float32
    tokens, tiles, region, routed = sizes(_B, _T, _D, _E, _H)

    def arr(name):
        return np.asarray(inputs[name])

    half = HEAD_DIM // 2
    inv_freq = f32(10000.0) ** (-np.arange(half, dtype=f32) / f32(half))
    angle = np.arange(_T, dtype=f32)[:, None] * inv_freq.astype(f32)[None, :]
    cos, sin = np.cos(angle), np.sin(angle)
    s, t = np.arange(P)[:, None], np.arange(P)[None, :]
    rep = lambda row: np.broadcast_to(np.asarray(row, f32).reshape(1, -1), (P, np.asarray(row).size))
    head = np.arange(P)[:, None] // HEAD_DIM == np.arange(P // HEAD_DIM)[None, :]
    consts_f = np.concatenate([
        s == t, s <= t, np.ones((P, P)), s // HEAD_DIM == t // HEAD_DIM, head,
        rep(np.arange(_E)), rep(np.arange(32) * P), rep(np.tril(np.ones((_E, _E)))),
        rep(np.arange(routed)), rep(np.arange(_E) * region), rep([-0.5])], axis=1).astype(f32)
    import ml_dtypes
    consts_b = np.concatenate([s < t, np.ones((P, P))], axis=1).astype(ml_dtypes.bfloat16)
    n = np.arange(tiles)
    token_ids = ((n % 2) * _T + (n // 2) * P)[None, :] + np.arange(P)[:, None]
    token_ids = np.concatenate([token_ids, tokens + np.arange(P)[:, None]], axis=1).astype(np.uint32)

    def chunked(w):
        e, o, i = w.shape
        return np.ascontiguousarray(w.transpose(2, 0, 1).reshape(i // P, P, e, o).transpose(1, 2, 0, 3).reshape(P, e, -1))

    arrays = {
        "x": arr("L0_attn_x").reshape(tokens, _D),
        "w_qk": np.ascontiguousarray(np.concatenate([arr("L0_attn_Wq").T, arr("L0_attn_Wk").T], axis=1)),
        "w_v": np.ascontiguousarray(arr("L0_attn_Wv").T),
        "w_o": np.ascontiguousarray(arr("L0_attn_Wo").T),
        "rope": np.concatenate([cos, cos, -sin, sin], axis=1).astype(f32),
        "norm_scale": arr("L0_ffn_norm_scale").reshape(1, _D),
        "w_router": np.ascontiguousarray(arr("L0_ffn_w_router").T),
        "w_up": chunked(arr("L0_ffn_w_up")),
        "w_down": chunked(arr("L0_ffn_w_down")),
        "consts_f": consts_f,
        "consts_b": consts_b,
        "token_ids": token_ids,
    }
    nc = bacc.Bacc("TRN2", target_bir_lowering=False, num_devices=1)
    aps = [nc.dram_tensor(k, a.shape, mybir.dt.from_np(a.dtype), kind="ExternalInput").ap() for k, a in arrays.items()]
    routed_rows = nc.dram_tensor("routed_rows", [_E * region + P, ROW], F32, kind="Internal").ap()
    out = nc.dram_tensor("out", [tokens + P, _D], F32, kind="ExternalOutput").ap()
    block_kernel(nc, *aps, routed_rows, out, _B, _T, _E, _H)
    r = run_bass_kernel_spmd(nc, [arrays], core_ids=[0])
    return np.asarray(r.results[0]["out"])[0:tokens].reshape(_B, _T, _D)
```

```python
from contextlib import ExitStack

import concourse.bass as bass
from concourse import mybir

P = 128
ALU = mybir.AluOpType
ACT = mybir.ActivationFunctionType
F32 = mybir.dt.float32
BF16 = mybir.dt.bfloat16
F16 = mybir.dt.float16
U32 = mybir.dt.uint32
AX_X = mybir.AxisListType.X

LN_EPS, RMS_EPS, DEN_EPS = 1e-5, 1e-6, 1e-6
HEAD_DIM = 16
ROW = 260
TOKEN, W_SECOND, W_GAP, FIRST_EXPERT = 256, 257, 258, 259
RING = 4
PIECE = 512

RANGE = 2.0 ** 15
LOW_SHIFT = 2.0 ** 12
SQUARES_FLOOR = 1e-12
EXPONENT_BITS = 0x7F800000


def sizes(batches, length, dim, experts, hidden):
    tokens = batches * length
    tiles = tokens // P
    region = tokens + P
    routed = (2 * tokens + experts * (P - 1)) // P
    return tokens, tiles, region, routed


def block_kernel(nc, x, w_qk, w_v, w_o, rope, norm_scale, w_router, w_up, w_down, consts_f, consts_b,
                 token_ids, routed_rows, out, batches, length, experts, hidden):
    dim = x.shape[1]
    tokens, tiles, region, routed_tiles = sizes(batches, length, dim, experts, hidden)
    per_batch = tiles // batches
    heads = dim // HEAD_DIM
    KC = dim // P
    HC = hidden // P
    pad_region = experts * region
    assert batches == 2 and KC == 2 and heads == 16 and tiles % RING == 0 and HC == 4
    assert experts == 8 and hidden == 512

    x_out = out[0:tokens, :]

    with ExitStack() as ctx:
        def sb(name, shape, dt=F32):
            return ctx.enter_context(nc.sbuf_tensor(name, shape, dt))

        def psum(name, shape):
            return ctx.enter_context(nc.psum_tensor(name, shape, F32))

        def sem(name):
            return ctx.enter_context(nc.semaphore(name))

        wqk_sb = sb("wqk_sb", [P, KC, 2 * dim])
        wv_sb = sb("wv_sb", [P, KC, dim])
        wo_sb = sb("wo_sb", [P, KC, dim])
        wr_sb = sb("wr_sb", [P, KC, experts])
        rope_sb = sb("rope_sb", [P, per_batch, 2 * HEAD_DIM])
        scale_sb = sb("scale_sb", [P, dim])
        up_pieces, down_pieces = experts * KC * 2, experts * HC * dim // PIECE
        up_sb = sb("up_sb", [P, up_pieces + 2, PIECE])
        up_of = up_sb[:, 0:up_pieces, :].rearrange("p (e j) n -> p e (j n)", e=experts)
        down_sb = sb("down_sb", [P, down_pieces + 2, PIECE])
        down_of = down_sb[:, 0:down_pieces, :].rearrange("p (e j) n -> p e (j n)", e=experts)
        down_small = sb("down_small", [P, down_pieces, PIECE], F16)
        down_small_of = down_small[:, :, :].rearrange("p (e j) n -> p e (j n)", e=experts)
        squares = sb("squares", [P, 2, experts])
        square_sum = sb("square_sum", [P, 2])
        norms2 = sb("norms2", [P, 3])
        inv_norms = sb("inv_norms", [P, 3])
        powers = sb("powers", [P, 3])
        w_scale = sb("w_scale", [P, 2])
        x_scale = sb("x_scale", [P, 1])
        up_scale = sb("up_scale", [P, 1])
        unscale = sb("unscale", [P, 1])
        hid_power = sb("hid_power", [P, 2])
        hid_scale = sb("hid_scale", [P, 1])
        down_scale = sb("down_scale", [P, 1])
        y_unscale = sb("y_unscale", [P, 1])
        scale_peak = sb("scale_peak", [P, 1])
        NF = consts_f.shape[1]
        cf = sb("cf", [P, NF])
        ident = cf[:, 0:P]
        causal = cf[:, P:2 * P]
        ones = cf[:, 2 * P:3 * P]
        same_head = cf[:, 3 * P:4 * P]
        at = 4 * P
        head_mask = cf[:, at:at + 8]
        at += 8
        expert_iota = cf[:, at:at + experts]
        at += experts
        tile_starts = cf[:, at:at + 32]
        at += 32
        low_tri = cf[:, at:at + experts * experts]
        at += experts * experts
        tile_iota = cf[:, at:at + routed_tiles]
        at += routed_tiles
        region_start = cf[:, at:at + experts]
        at += experts
        minus_half = cf[:, at:at + 1]
        at += 1
        assert at == NF
        cb = sb("cb", [P, 2 * P], BF16)
        earlier = cb[:, 0:P]
        ones_b = cb[:, P:2 * P]
        ids = sb("ids", [P, tiles + 1], U32)

        xin = sb("xin", [P, RING, dim])
        stats1 = sb("stats1", [P, 2, 6])
        mv1 = sb("mv1", [P, 2, 2])
        rstd1 = sb("rstd1", [P, 2, 1])
        xhat = sb("xhat", [P, 2, dim])
        xhatT = sb("xhatT", [P, 2, KC, P])
        rot_a = sb("rot_a", [P, 2 * dim])
        rot_b = sb("rot_b", [P, 2 * dim])
        rot = sb("rot", [P, 2 * dim])
        erot = sb("erot", [P, 2 * dim])
        rot1 = sb("rot1", [P, 2 * dim])
        phi = sb("phi", [P, 2, 2 * dim])
        v_pad = sb("v_pad", [P, 2, heads, 2 * HEAD_DIM])
        kacc = sb("kacc", [P, 2, dim])
        qk_prod = sb("qk_prod", [P, dim])
        den = sb("den", [P, heads])
        rden = sb("rden", [P, heads])
        qn = sb("qn", [P, dim])
        kT = sb("kT", [P, KC, P])
        qT = sb("qT", [P, KC, P])
        q_head = sb("q_head", [P, 8, KC, P])
        attn = sb("attn", [P, 4, 4, P])
        state = sb("state", [P, 2, KC, P])
        state_add = sb("state_add", [P, KC, P])
        yT = sb("yT", [P, KC, P])
        x1 = sb("x1", [P, dim])
        stats2 = sb("stats2", [P, 6])
        mv2 = sb("mv2", [P, 2])
        std2 = sb("std2", [P, 1])
        var1 = sb("var1", [P, 2, 1])
        var2 = sb("var2", [P, 2])
        inv2 = sb("inv2", [P, 2])
        rms2 = sb("rms2", [P, 1])
        xhat2 = sb("xhat2", [P, dim])
        acc = sb("acc", [P, RING, dim])
        rows = sb("rows", [P, RING, ROW])
        xnT = sb("xnT", [P, KC, P])
        scores8 = sb("scores8", [P, experts])
        top8 = sb("top8", [P, 8])
        top8_at = sb("top8_at", [P, 2, 8], U32)
        onehot = sb("onehot", [P, 2, 2, experts])
        gap = sb("gap", [P, 1])
        egap = sb("egap", [P, 1])
        gap1 = sb("gap1", [P, 1])
        w_first = sb("w_first", [P, 1])
        members = sb("members", [P, 2, experts], BF16)
        macc = sb("macc", [P, experts], BF16)
        rank_prod = sb("rank_prod", [P, 2, experts])
        rank = sb("rank", [P, 2])
        slot_of = sb("slot_of", [P, RING, 2], U32)

        cmp_c = sb("cmp_c", [P, experts, 32])
        counts = sb("counts", [P, experts])
        ntiles = sb("ntiles", [P, experts])
        cum_prod = sb("cum_prod", [P, experts, experts])
        cum = sb("cum", [P, experts])
        past, past_n = [b[:, :, :].rearrange("p u n -> p (u n)")[:, 0:routed_tiles * experts].rearrange(
            "p (t e) -> p t e", e=experts) for b in (phi, xin)]
        expert_f = sb("expert_f", [P, routed_tiles])
        next_region = sb("next_region", [P, experts])
        jumps = sb("jumps", [P, routed_tiles])
        start_f = sb("start_f", [P, routed_tiles])
        expert_u = sb("expert_u", [P, routed_tiles], U32)
        start_u = sb("start_u", [P, routed_tiles], U32)
        pad_u = sb("pad_u", [P, experts], U32)
        pad_rows = sb("pad_rows", [P, ROW])

        xr = sb("xr", [P, RING, ROW])
        is_first = sb("is_first", [P, 1])
        w_row = sb("w_row", [P, 2, 1])
        token_of = sb("token_of", [P, RING, 1], U32)
        free = attn[:, :, :, :].rearrange("p a h t -> p (a h t)")
        y = free[:, 0:RING * dim].rearrange("p (u n) -> p u n", u=RING)
        hid = free[:, RING * dim:RING * dim + 2 * hidden].rearrange("p (b n) -> p b n", b=2)
        free = q_head[:, :, :, :].rearrange("p a c t -> p (a c t)")
        sgate = free[:, 0:hidden]
        xT_high = free[:, hidden:hidden + dim].bitcast(F16).rearrange("p (b c t) -> p b c t", b=2, c=KC)
        xT_low = free[:, hidden + dim:hidden + 2 * dim].bitcast(F16).rearrange("p (b c t) -> p b c t", b=2, c=KC)
        at = hidden + 2 * dim
        hT_high = free[:, at:at + hidden // 2].bitcast(F16).rearrange("p (c t) -> p c t", c=HC)
        hT_low = free[:, at + hidden // 2:at + hidden].bitcast(F16).rearrange("p (c t) -> p c t", c=HC)

        bank = [psum(f"bank{k}", [P, 512]) for k in range(8)]
        ps_scores = bank[0:4]
        ps_num, ps_state = bank[0], bank[1]
        ps_qk, ps_xv, ps_qT, ps_small = bank[4], bank[5], bank[6], bank[7]

        consts_in = sem("consts_in")
        qkv_in = sem("qkv_in")
        weights_in = sem("weights_in")
        up_in = [sem(f"up_in{e}") for e in range(experts)]
        down_in = [sem(f"down_in{e}") for e in range(experts)]
        x_loaded = [sem(f"x_loaded{u}") for u in range(RING)]
        acc_stored = [sem(f"acc_stored{u}") for u in range(RING)]
        scattered = [sem(f"scattered{u}") for u in range(RING)]
        pads_stored = sem("pads_stored")
        spare_zeroed = sem("spare_zeroed")
        init_done = sem("init_done")
        stats1_ready = sem("stats1_ready")
        mv1_ready = sem("mv1_ready")
        rstd1_ready = sem("rstd1_ready")
        xhat_ready = sem("xhat_ready")
        xhatT_psum = sem("xhatT_psum")
        xhatT_ready = sem("xhatT_ready")
        qk_psum = sem("qk_psum")
        v_psum = sem("v_psum")
        v_ready = sem("v_ready")
        rot_parts_ready = sem("rot_parts_ready")
        rot_ready = sem("rot_ready")
        exp_ready = sem("exp_ready")
        phi_ready = sem("phi_ready")
        kcum_psum = sem("kcum_psum")
        kT_psum = sem("kT_psum")
        kT_ready = sem("kT_ready")
        kacc_ready = sem("kacc_ready")
        kcum_read = sem("kcum_read")
        den_step = sem("den_step")
        rden_ready = sem("rden_ready")
        qn_ready = sem("qn_ready")
        qT_psum = sem("qT_psum")
        q_head_ready = sem("q_head_ready")
        qT_ready = sem("qT_ready")
        scores_psum = sem("scores_psum")
        attn_dve = sem("attn_dve")
        attn_copied = sem("attn_copied")
        attn_pool = sem("attn_pool")
        num_psum = sem("num_psum")
        yT_ready = sem("yT_ready")
        state_psum = sem("state_psum")
        state_add_ready = sem("state_add_ready")
        state_ready = sem("state_ready")
        wo_psum = sem("wo_psum")
        x1_ready = sem("x1_ready")
        stats2_ready = sem("stats2_ready")
        mv2_ready = sem("mv2_ready")
        var1_ready = sem("var1_ready")
        var2_ready = sem("var2_ready")
        inv2_ready = sem("inv2_ready")
        std2_ready = sem("std2_ready")
        rms2_ready = sem("rms2_ready")
        xhat2_ready = sem("xhat2_ready")
        xn_ready = sem("xn_ready")
        acc_ready = sem("acc_ready")
        tok_ready = sem("tok_ready")
        xnT_psum = sem("xnT_psum")
        xnT_ready = sem("xnT_ready")
        logits_psum = sem("logits_psum")
        ranks_psum = sem("ranks_psum")
        route_step = sem("route_step")
        members_ready = sem("members_ready")
        gap_ready = sem("gap_ready")
        egap_ready = sem("egap_ready")
        meta_ready = sem("meta_ready")
        macc_ready = sem("macc_ready")
        rank_step = sem("rank_step")
        slots_ready = sem("slots_ready")
        squares_ready = sem("squares_ready")
        square_sum_ready = sem("square_sum_ready")
        norms_psum = sem("norms_psum")
        norms_ready = sem("norms_ready")
        inv_norms_ready = sem("inv_norms_ready")
        scale_step = sem("scale_step")
        high_ready = sem("high_ready")
        low_ready = sem("low_ready")
        down_high_ready = sem("down_high_ready")
        down_low_ready = sem("down_low_ready")
        down_small_ready = sem("down_small_ready")
        counts_psum = sem("counts_psum")
        table_step = sem("table_step")
        pads_ready = sem("pads_ready")
        expert_step = sem("expert_step")
        table_ready = sem("table_ready")
        rows_loaded = [sem(f"rows_loaded{u}") for u in range(RING)]
        xrT_psum = sem("xrT_psum")
        xT_high_ready = sem("xT_high_ready")
        xT_low_ready = sem("xT_low_ready")
        gate_psum = sem("gate_psum")
        up_psum = sem("up_psum")
        sgate_ready = sem("sgate_ready")
        hid_ready = sem("hid_ready")
        hidT_psum = sem("hidT_psum")
        hT_high_ready = sem("hT_high_ready")
        hT_low_ready = sem("hT_low_ready")
        down_psum = sem("down_psum")
        w_step = sem("w_step")
        y_ready = sem("y_ready")
        added = sem("added")

        block = ctx.enter_context(nc.Block())

        def alive(n):
            return not isinstance(n, int) or 0 <= n < tiles

        def over_tiles(eng, step):
            for n in range(-3, 3 * RING):
                step(n, n % RING)
            with eng.Fori(3, tiles // RING - 1) as group:
                for u in range(RING):
                    step(group * RING + u, u)
            for n in range(tiles - RING, tiles + 4):
                step(n, n % RING)

        ps_gate, ps_up = [bank[0], bank[1]], [bank[2], bank[3]]
        ps_xrT, ps_hidT, ps_down = bank[4], bank[5], [bank[6], bank[7]]

        def piece_of(n, k):
            return (n - 3 * RING) * 2 + k

        assert 2 * (tiles - 4 * RING) == up_pieces and down_pieces == 16

        def down_pieces_of(n):
            if not isinstance(n, int) or n < tiles - RING:
                return [], []
            k = n - (tiles - RING)
            return ([2 * k], [2 * k + 1]) if k < RING else ([], [RING + k])

        down_low_behind = range(2 * RING + 2, 3 * RING)
        down_pieces_last = range(3 * RING, down_pieces)

        def alive2(t):
            return not isinstance(t, int) or 0 <= t < routed_tiles

        def over_routed(eng, step):
            body = 2 * RING
            whole = routed_tiles // body
            for t in range(-1, body):
                step(t, t % RING)
            with eng.Fori(1, whole) as group:
                for k in range(body):
                    step(group * body + k, k % RING)
            for t in range(whole * body, routed_tiles + 1):
                step(t, t % RING)

        def settle(eng):
            eng.nop(nofuse=True)

        def first_round(n):
            return isinstance(n, int) and n < RING

        def later(n, k=1):
            return not isinstance(n, int) or n >= k

        def store_pads(eng, some):
            eng.wait_ge(pads_ready, 1)
            for e in some:
                at_row = eng.value_load(pad_u[0:1, e:e + 1], min_val=0, max_val=pad_region - P)
                eng.dma_start(routed_rows[bass.ds(at_row, P), :], pad_rows[:, :]).then_inc(pads_stored, 16)

        @block.sync
        def _(sp):
            def x_rows(n, u):
                return bass.ds((u % 2) * length + (n - u % 2) // 2 * P, P)

            def load_x(n, u):
                sp.dma_start(xin[:, u, :], x[x_rows(n, u), :]).then_inc(x_loaded[u], 16)

            load_x(0, 0)
            sp.dma_start(wqk_sb[:, :, :], w_qk.rearrange("(c p) n -> p c n", p=P)).then_inc(qkv_in, 16)
            load_x(1, 1)
            sp.dma_start(rope_sb[:, :, :], rope.rearrange("p (i n) -> p i n", n=2 * HEAD_DIM)).then_inc(weights_in, 16)
            sp.dma_start(ids[:, :], token_ids).then_inc(weights_in, 16)
            load_x(2, 2)
            load_x(3, 3)
            sp.wait_ge(table_step, 2)
            sp.dma_start(routed_rows[pad_region:pad_region + P, :], pad_rows[:, :]).then_inc(pads_stored, 16)

            def step(n, u):
                m, um = n - 1, (u + 3) % RING
                if alive(m):
                    if not isinstance(m, int) or m + RING < tiles:
                        sp.wait_ge(x1_ready, m + 1)
                        load_x(m + RING, um)
                    sp.wait_ge(acc_ready, m + 1)
                    sp.dma_start(x_out[x_rows(m, um), :], acc[:, um, :]).then_inc(acc_stored[um], 16)

            over_tiles(sp, step)

            store_pads(sp, range(0, experts // 2))
            sp.wait_ge(table_ready, 1)
            sp.wait_ge(pads_stored, 16 * (experts + 1))
            for u in range(RING):
                sp.wait_ge(scattered[u], 32 * (tiles // RING))

            def load_rows(t, u):
                if not (isinstance(t, int) and t < RING):
                    sp.wait_ge(w_step, 3 * (t - RING + 1))
                start = sp.value_load(start_u[0:1, t:t + 1] if isinstance(t, int) else start_u[0:1, bass.ds(t, 1)],
                                      min_val=0, max_val=pad_region)
                sp.dma_start(xr[:, u, :], routed_rows[bass.ds(start, P), :]).then_inc(rows_loaded[u], 16)

            whole = routed_tiles // RING
            for t in range(RING):
                load_rows(t, t)
            with sp.Fori(1, whole) as group:
                for u in range(RING):
                    load_rows(group * RING + u, u)
            for t in range(whole * RING, routed_tiles):
                load_rows(t, t % RING)

        @block.scalar
        def _(act):
            act.dma_start(cf[:, :], consts_f).then_inc(consts_in, 16)
            act.dma_start(wv_sb[:, :, :], w_v.rearrange("(c p) n -> p c n", p=P)).then_inc(qkv_in, 16)
            act.dma_start(wo_sb[:, :, :], w_o.rearrange("(c p) n -> p c n", p=P)).then_inc(weights_in, 16)
            act.dma_start(wr_sb[:, :, :], w_router.rearrange("(c p) n -> p c n", p=P)).then_inc(weights_in, 16)
            act.dma_start(cb[:, :], consts_b).then_inc(weights_in, 16)
            act.dma_start(scale_sb[:, :], norm_scale.to_broadcast([P, dim])).then_inc(weights_in, 16)
            act.wait_ge(init_done, 4)
            act.wait_ge(consts_in, 16)

            def load_up(e):
                at0 = 2 + e * KC * 2
                act.dma_start(up_sb[:, at0:at0 + KC * 2, :],
                              w_up[:, e, :].rearrange("p (j n) -> p j n", n=PIECE)).then_inc(up_in[e], 16)

            def load_down(e):
                at0 = 2 + e * 2
                act.dma_start(down_sb[:, at0:at0 + 2, :],
                              w_down[:, e, :].rearrange("p (j n) -> p j n", n=PIECE)).then_inc(down_in[e], 16)

            unused = xr[:, :, :].rearrange("p u n -> p (u n)").bitcast(BF16)

            def up_squares(e):
                act.wait_ge(up_in[e], 16)
                if e > 0:
                    act.wait_ge(squares_ready, 2 * e)
                nc.scalar.activation(unused[:, 0:KC * 2 * PIECE],
                                     up_sb[:, 2 + e * KC * 2:2 + (e + 1) * KC * 2, :].rearrange("p j n -> p (j n)"),
                                     ACT.Square, accum_out=squares[:, 0, e:e + 1]).then_inc(squares_ready, 1)

            def down_squares(e):
                act.wait_ge(down_in[e], 16)
                act.wait_ge(squares_ready, 2 * e + 1)
                nc.scalar.activation(unused[:, 0:2 * PIECE],
                                     down_sb[:, 2 + e * 2:4 + e * 2, :].rearrange("p j n -> p (j n)"),
                                     ACT.Square, accum_out=squares[:, 1, e:e + 1]).then_inc(squares_ready, 1)

            def split_high(p):
                act.wait_ge(low_ready, p + 1)
                nc.scalar.activation(up_sb[:, bass.ds(p, 1), :].rearrange("p j n -> p (j n)").bitcast(F16)[:, 0:PIECE],
                                     up_sb[:, bass.ds(p + 2, 1), :].rearrange("p j n -> p (j n)"),
                                     ACT.Copy, scale=w_scale[:, 0:1]).then_inc(high_ready, 1)

            def split_down_high(p):
                act.wait_ge(down_low_ready, p + 1)
                high = down_sb[:, p, :].bitcast(F16)[:, 0:PIECE]
                nc.scalar.activation(high, down_sb[:, p + 2, :], ACT.Copy,
                                     scale=w_scale[:, 1:2]).then_inc(down_high_ready, 1)
                act.wait_ge(down_high_ready, p + 1)
                nc.scalar.activation(down_small[:, p, :], high, ACT.Copy, scale=1 / LOW_SHIFT).then_inc(down_small_ready, 1)

            def step(n, u):
                m, x = n + 1, n + 2
                nb = (u + 1) % 2
                early, late = down_pieces_of(n)
                if isinstance(n, int) and 0 <= n < experts:
                    if n == 0:
                        load_up(0)
                        load_down(0)
                    else:
                        up_squares(n - 1)
                    if n < experts - 1:
                        load_up(n + 1)
                        load_down(n + 1)
                if not isinstance(n, int):
                    split_high(piece_of(n, 0))
                    split_high(piece_of(n, 1))
                for p in early:
                    split_down_high(p)
                if alive(n):
                    act.wait_ge(qT_psum, n + 1)
                    if later(n):
                        act.wait_ge(num_psum, n)
                    for j in range(8):
                        nc.scalar.activation(q_head[:, j, :, :],
                                             ps_qT[:, 0:dim].rearrange("p (c t) -> p c t", c=KC),
                                             ACT.Copy, scale=head_mask[:, j:j + 1]).then_inc(q_head_ready, 1)
                    nc.scalar.activation(qT[:, :, :], ps_qT[:, 0:dim], ACT.Copy).then_inc(qT_ready, 1)
                if alive(m):
                    act.wait_ge(v_psum, m + 1)
                    if later(m, 2):
                        act.wait_ge(state_psum, m - 1)
                    nc.scalar.activation(
                        v_pad[:, nb, :, :].rearrange("p (a b) (c d) -> p a (b c) d", b=2, c=2)[:, :, 0:4:3, :],
                        ps_xv[:, dim:2 * dim], ACT.Copy).then_inc(v_ready, 1)
                if alive(n - 3):
                    act.wait_ge(gap_ready, n - 2)
                    if later(n - 3):
                        act.wait_ge(meta_ready, 3 * (n - 3))
                    nc.scalar.activation(egap[:, :], gap[:, :], ACT.Exp).then_inc(egap_ready, 1)
                    act.wait_ge(egap_ready, 2 * (n - 3) + 1)
                    nc.scalar.activation(gap1[:, :], egap[:, :], ACT.Copy, bias=1.0).then_inc(egap_ready, 1)
                if alive(n):
                    act.wait_ge(scores_psum, 4 * n + 2)
                    nc.scalar.activation(attn[:, 1, :, :], ps_scores[1][:, :], ACT.Copy).then_inc(attn_copied, 1)
                if alive(m):
                    act.wait_ge(rot_ready, m + 1)
                    if later(m):
                        act.wait_ge(phi_ready, m)
                    nc.scalar.activation(erot[:, :], rot[:, :], ACT.Exp).then_inc(exp_ready, 1)
                    nc.scalar.activation(rot1[:, :], rot[:, :], ACT.Copy, bias=1.0).then_inc(exp_ready, 1)
                if alive(n - 2):
                    act.wait_ge(xnT_psum, n - 1)
                    if later(n - 2):
                        act.wait_ge(logits_psum, n - 2)
                    nc.scalar.activation(xnT[:, :, :], ps_xv[:, 0:dim], ACT.Copy).then_inc(xnT_ready, 1)
                if alive(x):
                    act.wait_ge(xhatT_psum, x + 1)
                    if later(x, 2):
                        act.wait_ge(v_psum, x - 1)
                    nc.scalar.activation(xhatT[:, u % 2, :, :], ps_qT[:, dim:2 * dim], ACT.Copy).then_inc(xhatT_ready, 1)
                for p in late:
                    split_down_high(p)
                if isinstance(n, int) and 0 < n < experts:
                    down_squares(n - 1)
                if isinstance(n, int) and n == experts - 1:
                    up_squares(n)
                    down_squares(n)
                if alive(n):
                    act.wait_ge(num_psum, n + 1)
                    if later(n):
                        act.wait_ge(wo_psum, n)
                    nc.scalar.activation(yT[:, :, :], ps_num[:, 0:dim], ACT.Copy).then_inc(yT_ready, 1)
                if alive(m):
                    act.wait_ge(kT_psum, m + 1)
                    nc.scalar.activation(kT[:, :, :], ps_xv[:, dim:2 * dim], ACT.Copy).then_inc(kT_ready, 1)

            over_tiles(act, step)
            store_pads(act, range(experts // 2, experts))
            for p in down_pieces_last:
                split_down_high(p)

            def step2(t, u):
                b = u % 2
                if alive2(t + 1):
                    act.wait_ge(xrT_psum, t + 2)
                    nc.scalar.activation(xT_high[:, 1 - b, :, :], ps_xrT[:, 0:dim], ACT.Copy,
                                         scale=x_scale[:, :]).then_inc(xT_high_ready, 1)
                if alive2(t - 1):
                    act.wait_ge(hidT_psum, t)
                    nc.scalar.activation(hT_high, ps_hidT[:, :], ACT.Copy, scale=1 / LOW_SHIFT).then_inc(hT_high_ready, 1)
                if alive2(t):
                    act.wait_ge(gate_psum, t + 1)
                    if not (isinstance(t, int) and t < 1):
                        act.wait_ge(hid_ready, t)
                    nc.scalar.activation(sgate, ps_gate[b][:, :], ACT.Silu,
                                         scale=unscale[:, :]).then_inc(sgate_ready, 1)

            over_routed(act, step2)

        @block.vector
        def _(dve):
            nc.vector.memset(v_pad[:, :, :, :], 0.0).then_inc(init_done, 1)
            nc.vector.memset(pad_rows[:, :], 0.0).then_inc(table_step, 1)

            def weights_here():
                dve.wait_ge(consts_in, 16)
                dve.wait_ge(weights_in, 16 * 6)
                dve.wait_ge(table_step, 1)
                nc.vector.tensor_copy(pad_rows[:, TOKEN:TOKEN + 1].bitcast(U32),
                                      ids[:, tiles:tiles + 1]).then_inc(table_step, 1)

            def stats_first(n, u):
                dve.wait_ge(x_loaded[u], 4 * (n - u) + 16)
                if later(n, 2):
                    dve.wait_ge(mv1_ready, n - 1)
                nc.vector.bn_stats(stats1[:, u % 2, :], xin[:, u, :]).then_inc(stats1_ready, 1)

            def moments_first(n, u):
                b = u % 2
                dve.wait_ge(stats1_ready, n + 1)
                if later(n, 2):
                    dve.wait_ge(xhat_ready, n - 1)
                settle(dve)
                nc.vector.bn_aggr(mv1[:, b, :], stats1[:, b, :]).then_inc(mv1_ready, 1)

            def variance_first(n, u):
                b = u % 2
                dve.wait_ge(mv1_ready, n + 1)
                if later(n, 2):
                    dve.wait_ge(rstd1_ready, n - 1)
                nc.vector.tensor_scalar(var1[:, b, :], mv1[:, b, 1:2], LN_EPS, None, ALU.add).then_inc(var1_ready, 1)

            def norm1(n, u):
                b = u % 2
                dve.wait_ge(rstd1_ready, n + 1)
                dve.wait_ge(mv1_ready, n + 1)
                if later(n, 2):
                    dve.wait_ge(xhatT_psum, n - 1)
                nc.vector.tensor_scalar(xhat[:, b, :], xin[:, u, :], mv1[:, b, 0:1], rstd1[:, b, :],
                                        ALU.subtract, ALU.mult).then_inc(xhat_ready, 1)

            def mask(n, g):
                if later(n):
                    dve.wait_ge(num_psum, n)
                dve.wait_ge(scores_psum, 4 * n + g + 1)
                nc.vector.tensor_tensor(attn[:, g, :, :], ps_scores[g][:, :].rearrange("p (h t) -> p h t", h=4),
                                        causal.unsqueeze(1).to_broadcast([P, 4, P]), ALU.mult).then_inc(attn_dve, 1)

            half = HEAD_DIM // 2

            def rope_table(n, u):
                i = (n - u % 2) // 2
                return rope_sb[:, bass.ds(i, 1), :].rearrange("p i n -> p (i n)")

            def rotate_cos(n, u):
                cos = rope_table(n, u)[:, 0:HEAD_DIM].unsqueeze(1).to_broadcast([P, 2 * heads, HEAD_DIM])
                dve.wait_ge(qk_psum, n + 1)
                if later(n):
                    dve.wait_ge(rot_ready, n)
                nc.vector.tensor_tensor(rot_a[:, :].rearrange("p (h d) -> p h d", d=HEAD_DIM),
                                        ps_qk[:, :].rearrange("p (h d) -> p h d", d=HEAD_DIM), cos,
                                        ALU.mult).then_inc(rot_parts_ready, 1)

            def rotate_sin(n, u, k):
                sin = rope_table(n, u)[:, HEAD_DIM + k * half:HEAD_DIM + (k + 1) * half].unsqueeze(1)
                qk = ps_qk[:, :].rearrange("p (h d) -> p h d", d=HEAD_DIM)
                nc.vector.tensor_tensor(rot_b[:, :].rearrange("p (h d) -> p h d", d=HEAD_DIM)[:, :, k * half:(k + 1) * half],
                                        qk[:, :, (1 - k) * half:(2 - k) * half],
                                        sin.to_broadcast([P, 2 * heads, half]), ALU.mult).then_inc(rot_parts_ready, 1)

            def features(n, u):
                dve.wait_ge(exp_ready, 2 * n + 2)
                if later(n, 2):
                    dve.wait_ge(state_psum, n - 1)
                nc.vector.scalar_tensor_tensor(phi[:, u % 2, :], erot[:, :], 1.0, rot1[:, :], ALU.min,
                                               ALU.max).then_inc(phi_ready, 1)

            def state_part(n, u):
                dve.wait_ge(state_psum, n + 1)
                if later(n):
                    dve.wait_ge(state_ready, n)
                nc.vector.tensor_tensor(state_add[:, :, :],
                                        ps_state[:, 0:dim].rearrange("p (c t) -> p c t", c=KC),
                                        same_head.unsqueeze(1).to_broadcast([P, KC, P]),
                                        ALU.mult).then_inc(state_add_ready, 1)

            def key_products(n, u):
                dve.wait_ge(kcum_psum, n + 1)
                dve.wait_ge(phi_ready, n + 1)
                nc.vector.tensor_tensor(qk_prod[:, :], ps_small[:, 0:dim], phi[:, u % 2, 0:dim],
                                        ALU.mult).then_inc(kcum_read, 1)

            def key_sums(n):
                dve.wait_ge(kcum_read, n + 1)
                nc.vector.tensor_reduce(den[:, :], qk_prod[:, :].rearrange("p (h d) -> p h d", d=HEAD_DIM),
                                        AX_X, ALU.add).then_inc(den_step, 1)

            def denominators(n):
                dve.wait_ge(den_step, 2 * n + 1)
                nc.vector.tensor_scalar(den[:, :], den[:, :], DEN_EPS, None, ALU.max).then_inc(den_step, 1)
                dve.wait_ge(den_step, 2 * n + 2)
                if later(n):
                    dve.wait_ge(qn_ready, n)
                nc.vector.reciprocal(rden[:, :], den[:, :]).then_inc(rden_ready, 1)

            def residual(n, u):
                dve.wait_ge(wo_psum, n + 1)
                if later(n):
                    dve.wait_ge(acc_ready, n)
                    dve.wait_ge(xhat2_ready, n)
                nc.vector.tensor_tensor(x1[:, :], ps_small[:, 0:dim], xin[:, u, :], ALU.add).then_inc(x1_ready, 1)

            def stats_second(n):
                dve.wait_ge(x1_ready, n + 1)
                nc.vector.bn_stats(stats2[:, :], x1[:, :]).then_inc(stats2_ready, 1)

            def moments_second(n):
                dve.wait_ge(stats2_ready, n + 1)
                settle(dve)
                nc.vector.bn_aggr(mv2[:, :], stats2[:, :]).then_inc(mv2_ready, 1)

            def variances_second(n):
                dve.wait_ge(mv2_ready, n + 1)
                if later(n):
                    dve.wait_ge(inv2_ready, n)
                nc.vector.tensor_scalar(var2[:, 0:1], mv2[:, 1:2], LN_EPS, None, ALU.add).then_inc(var2_ready, 1)
                nc.vector.tensor_scalar(var2[:, 1:2], mv2[:, 1:2], 1.0 + RMS_EPS, LN_EPS * RMS_EPS, ALU.mult,
                                        ALU.add).then_inc(var2_ready, 1)

            def norm2(n):
                dve.wait_ge(inv2_ready, n + 1)
                nc.vector.tensor_tensor(std2[:, :], var2[:, 0:1], inv2[:, 0:1], ALU.mult).then_inc(std2_ready, 1)
                nc.vector.tensor_scalar(xhat2[:, :], x1[:, :], mv2[:, 0:1], inv2[:, 0:1],
                                        ALU.subtract, ALU.mult).then_inc(xhat2_ready, 1)
                dve.wait_ge(std2_ready, n + 1)
                nc.vector.tensor_tensor(rms2[:, :], std2[:, :], inv2[:, 1:2], ALU.mult).then_inc(rms2_ready, 1)

            def expert_input(n, u):
                dve.wait_ge(xhat2_ready, n + 1)
                dve.wait_ge(rms2_ready, n + 1)
                if not first_round(n):
                    dve.wait_ge(scattered[u], 8 * (n - u))
                nc.vector.scalar_tensor_tensor(rows[:, u, 0:dim], xhat2[:, :], rms2[:, :], scale_sb[:, :],
                                               ALU.mult, ALU.mult).then_inc(xn_ready, 1)

            def copy_logits(n):
                dve.wait_ge(logits_psum, n + 1)
                nc.vector.tensor_copy(scores8[:, :], ps_small[:, 256:256 + experts]).then_inc(route_step, 1)

            def top_values(n):
                dve.wait_ge(route_step, 5 * n + 1)
                settle(dve)
                nc.vector.max(top8[:, :], scores8[:, :]).then_inc(route_step, 1)

            def top_gap(n):
                dve.wait_ge(route_step, 5 * n + 2)
                if later(n):
                    dve.wait_ge(egap_ready, 2 * n)
                nc.vector.tensor_tensor(gap[:, :], top8[:, 1:2], top8[:, 0:1], ALU.subtract).then_inc(gap_ready, 1)

            def top_experts(n, u):
                nc.vector.max_index(top8_at[:, u % 2, :], top8[:, :], scores8[:, :]).then_inc(route_step, 1)

            def one_hots(n, u):
                b = u % 2
                dve.wait_ge(route_step, 5 * n + 3)
                nc.vector.tensor_tensor(
                    onehot[:, b, :, :], expert_iota.unsqueeze(1).to_broadcast([P, 2, experts]),
                    top8_at[:, b, 0:2].unsqueeze(2).to_broadcast([P, 2, experts]), ALU.is_equal).then_inc(route_step, 1)

            def member_rows(n, u):
                b = u % 2
                dve.wait_ge(route_step, 5 * n + 4)
                if later(n, 2):
                    dve.wait_ge(macc_ready, n - 1)
                nc.vector.tensor_tensor(members[:, b, :], onehot[:, b, 0, :], onehot[:, b, 1, :],
                                        ALU.add).then_inc(members_ready, 1)

            def first_weight(n):
                dve.wait_ge(egap_ready, 2 * n + 2)
                nc.vector.reciprocal(w_first[:, :], gap1[:, :]).then_inc(route_step, 1)

            def second_weight(n, u):
                dve.wait_ge(route_step, 5 * n + 5)
                nc.vector.tensor_tensor(rows[:, u, W_SECOND:W_SECOND + 1], w_first[:, :], egap[:, :],
                                        ALU.mult).then_inc(meta_ready, 1)

            def weight_gap(n, u):
                dve.wait_ge(meta_ready, 3 * n + 1)
                nc.vector.tensor_tensor(rows[:, u, W_GAP:W_GAP + 1], w_first[:, :],
                                        rows[:, u, W_SECOND:W_SECOND + 1], ALU.subtract).then_inc(meta_ready, 1)
                nc.vector.tensor_copy(rows[:, u, FIRST_EXPERT:FIRST_EXPERT + 1],
                                      top8_at[:, u % 2, 0:1]).then_inc(meta_ready, 1)

            def rank_products(n, u):
                dve.wait_ge(ranks_psum, n + 1)
                nc.vector.tensor_tensor(
                    rank_prod[:, :, :], ps_small[:, 264:264 + experts].unsqueeze(1).to_broadcast([P, 2, experts]),
                    onehot[:, u % 2, :, :], ALU.mult).then_inc(rank_step, 1)

            def rank_sums(n):
                dve.wait_ge(rank_step, 2 * n + 1)
                nc.vector.tensor_reduce(rank[:, :], rank_prod[:, :, :], AX_X, ALU.add).then_inc(rank_step, 1)

            def places(n, u):
                dve.wait_ge(rank_step, 2 * n + 2)
                if not first_round(n):
                    dve.wait_ge(scattered[u], 8 * (n - u))
                nc.vector.scalar_tensor_tensor(slot_of[:, u, :], top8_at[:, u % 2, 0:2], float(region), rank[:, :],
                                               ALU.mult, ALU.add).then_inc(slots_ready, 1)

            def sums_of_squares():
                scale2 = cmp_c[:, :, :].rearrange("p e k -> p (e k)")[:, 0:dim]
                nc.vector.tensor_tensor(scale2, scale_sb[:, :], scale_sb[:, :], ALU.mult).then_inc(scale_step, 1)
                dve.wait_ge(squares_ready, 2 * experts)
                nc.vector.tensor_reduce(square_sum[:, :], squares[:, :, :], AX_X, ALU.add).then_inc(square_sum_ready, 1)
                dve.wait_ge(scale_step, 1)
                nc.vector.tensor_reduce(scale_peak[:, :], scale2, AX_X, ALU.max).then_inc(scale_step, 1)

            def bound_norms():
                dve.wait_ge(norms_psum, 1)
                nc.vector.tensor_scalar(norms2[:, 0:2], ps_small[:, 280:282], SQUARES_FLOOR, None,
                                        ALU.max).then_inc(norms_ready, 1)
                dve.wait_ge(scale_step, 2)
                nc.vector.tensor_scalar(norms2[:, 2:3], scale_peak[:, :], dim + 1.0, SQUARES_FLOOR, ALU.mult,
                                        ALU.max).then_inc(norms_ready, 1)

            def scale_done(count, ins):
                ins.then_inc(scale_step, 1)
                dve.wait_ge(scale_step, count)

            def take_scales():
                dve.wait_ge(inv_norms_ready, 1)
                scale_done(3, nc.vector.tensor_scalar(powers[:, :].bitcast(U32), inv_norms[:, :].bitcast(U32),
                                                      EXPONENT_BITS, None, ALU.bitwise_and))
                nc.vector.tensor_scalar(w_scale[:, :], powers[:, 0:2], RANGE, None, ALU.mult).then_inc(low_ready, 2)

            def take_hidden_scales():
                nc.vector.tensor_scalar(x_scale[:, :], powers[:, 2:3], RANGE, None, ALU.mult).then_inc(scale_step, 1)
                scale_done(5, nc.vector.tensor_tensor(hid_power[:, 0:1], powers[:, 0:1], powers[:, 2:3], ALU.mult))
                dve.wait_ge(low_ready, 2)
                nc.vector.tensor_tensor(up_scale[:, :], w_scale[:, 0:1], x_scale[:, :], ALU.mult).then_inc(scale_step, 1)
                scale_done(7, nc.vector.tensor_tensor(hid_power[:, 1:2], hid_power[:, 0:1], hid_power[:, 0:1], ALU.mult))
                nc.vector.scalar_tensor_tensor(down_scale[:, :], hid_power[:, 1:2], RANGE, w_scale[:, 1:2],
                                               ALU.mult, ALU.mult).then_inc(scale_step, 1)
                scale_done(9, nc.vector.reciprocal(unscale[:, :], up_scale[:, :]))
                nc.vector.scalar_tensor_tensor(hid_scale[:, :], hid_power[:, 1:2], RANGE * LOW_SHIFT, unscale[:, :],
                                               ALU.mult, ALU.mult).then_inc(scale_step, 1)
                nc.vector.reciprocal(y_unscale[:, :], down_scale[:, :]).then_inc(down_low_ready, 2)

            def split_down_low(p):
                dve.wait_ge(down_high_ready, p + 1)
                parts = down_sb[:, p, :].bitcast(F16)
                nc.vector.scalar_tensor_tensor(parts[:, PIECE:2 * PIECE], down_sb[:, p + 2, :], w_scale[:, 1:2],
                                               parts[:, 0:PIECE], ALU.mult, ALU.subtract).then_inc(down_low_ready, 1)

            def split_low(p):
                dve.wait_ge(high_ready, p + 1)
                parts = up_sb[:, bass.ds(p, 1), :].rearrange("p j n -> p (j n)").bitcast(F16)
                nc.vector.scalar_tensor_tensor(parts[:, PIECE:2 * PIECE],
                                               up_sb[:, bass.ds(p + 2, 1), :].rearrange("p j n -> p (j n)"),
                                               w_scale[:, 0:1], parts[:, 0:PIECE], ALU.mult,
                                               ALU.subtract).then_inc(low_ready, 1)

            def step(n, u):
                m, a, r = n + 1, n - 1, n - 3
                um, ua, ur = (u + 1) % RING, (u + 3) % RING, (u + 1) % RING
                if isinstance(n, int) and n == -1:
                    weights_here()
                if isinstance(n, int) and n == experts:
                    sums_of_squares()
                if isinstance(n, int) and n == experts + 3:
                    take_scales()
                if alive(r):
                    copy_logits(r)
                if alive(m):
                    rotate_cos(m, um)
                if alive(n + 2):
                    variance_first(n + 2, (u + 2) % RING)
                if alive(m):
                    rotate_sin(m, um, 0)
                if alive(r):
                    top_values(r)
                if alive(m):
                    rotate_sin(m, um, 1)
                if alive(r):
                    top_gap(r)
                    top_experts(r, ur)
                if not isinstance(n, int):
                    split_low(piece_of(n, 0))
                for p in down_pieces_of(n)[0]:
                    split_down_low(p)
                if alive(a):
                    residual(a, ua)
                if alive(r):
                    one_hots(r, ur)
                if alive(a):
                    stats_second(a)
                if alive(r):
                    member_rows(r, ur)
                if alive(n):
                    mask(n, 0)
                if alive(a):
                    moments_second(a)
                if alive(n + 2):
                    norm1(n + 2, (u + 2) % RING)
                if alive(a):
                    variances_second(a)
                if not isinstance(n, int):
                    split_low(piece_of(n, 1))
                if alive(n):
                    mask(n, 2)
                    mask(n, 3)
                if alive(r):
                    rank_products(r, ur)
                    first_weight(r)
                if isinstance(n, int) and n == experts + 1:
                    bound_norms()
                if alive(m):
                    features(m, um)
                if alive(r):
                    rank_sums(r)
                    second_weight(r, ur)
                if alive(a):
                    norm2(a)
                if alive(r):
                    weight_gap(r, ur)
                if alive(n):
                    state_part(n, u)
                if alive(a):
                    expert_input(a, ua)
                if alive(m):
                    key_products(m, um)
                if alive(r):
                    places(r, ur)
                if alive(m):
                    key_sums(m)
                if alive(m):
                    denominators(m)
                if alive(n + 3):
                    stats_first(n + 3, (u + 3) % RING)
                for p in down_pieces_of(n)[1]:
                    if p not in down_low_behind:
                        split_down_low(p)
                if isinstance(n, int) and n == experts + 3:
                    take_hidden_scales()
                if alive(n + 3):
                    moments_first(n + 3, (u + 3) % RING)

            over_tiles(dve, step)

            done = [2]

            def link(ins):
                done[0] += 1
                ins.then_inc(table_step, 1)
                dve.wait_ge(table_step, done[0])

            NT = routed_tiles
            dve.wait_ge(counts_psum, 1)
            link(nc.vector.tensor_copy(counts[:, :], ps_small[:, 272:272 + experts]))
            nc.vector.tensor_tensor(pad_u[:, :], region_start, counts[:, :], ALU.add).then_inc(pads_ready, 1)
            for p in down_low_behind:
                split_down_low(p)
            link(nc.vector.tensor_tensor(cmp_c[:, :, :], counts[:, :].unsqueeze(2).to_broadcast([P, experts, 32]),
                                         tile_starts.unsqueeze(1).to_broadcast([P, experts, 32]), ALU.is_gt))
            link(nc.vector.tensor_reduce(ntiles[:, :], cmp_c[:, :, :], AX_X, ALU.add))
            link(nc.vector.tensor_tensor(cum_prod[:, :, :], low_tri.rearrange("p (e f) -> p e f", e=experts),
                                         ntiles[:, :].unsqueeze(1).to_broadcast([P, experts, experts]), ALU.mult))
            nc.vector.tensor_scalar(next_region[:, :], ntiles[:, :], -float(P), float(region), ALU.mult,
                                    ALU.add).then_inc(expert_step, 1)
            link(nc.vector.tensor_reduce(cum[:, :], cum_prod[:, :, :], AX_X, ALU.add))
            link(nc.vector.tensor_tensor(past[:, :, :], tile_iota.unsqueeze(2).to_broadcast([P, NT, experts]),
                                         cum[:, :].unsqueeze(1).to_broadcast([P, NT, experts]), ALU.is_ge))
            nc.vector.tensor_reduce(expert_f[:, :], past[:, :, :], AX_X, ALU.add).then_inc(expert_step, 1)
            dve.wait_ge(expert_step, 2)
            link(nc.vector.tensor_tensor(past_n[:, :, :], past[:, :, :],
                                         next_region[:, :].unsqueeze(1).to_broadcast([P, NT, experts]), ALU.mult))
            link(nc.vector.tensor_reduce(jumps[:, :], past_n[:, :, :], AX_X, ALU.add))
            link(nc.vector.scalar_tensor_tensor(start_f[:, :], tile_iota, float(P), jumps[:, :], ALU.mult, ALU.add))
            nc.vector.tensor_scalar(start_u[:, :], start_f[:, :], float(pad_region), None, ALU.min).then_inc(table_ready, 1)
            link(nc.vector.tensor_scalar(expert_f[:, :], expert_f[:, :], float(experts - 1), None, ALU.min))
            nc.vector.tensor_copy(expert_u[:, :], expert_f[:, :]).then_inc(table_ready, 1)

            for p in down_pieces_last:
                split_down_low(p)

            def rows_low(t, u):
                b = u % 2
                dve.wait_ge(xT_high_ready, t + 1)
                nc.vector.scalar_tensor_tensor(xT_low[:, b, :, :], ps_xrT[:, 0:dim].rearrange("p (c t) -> p c t", c=KC),
                                               x_scale[:, :], xT_high[:, b, :, :], ALU.mult,
                                               ALU.subtract).then_inc(xT_low_ready, 1)

            def hidden_product(t, u):
                b = u % 2
                dve.wait_ge(up_psum, t + 1)
                dve.wait_ge(sgate_ready, t + 1)
                if not (isinstance(t, int) and t < 2):
                    dve.wait_ge(hidT_psum, t - 1)
                nc.vector.scalar_tensor_tensor(hid[:, b, :], ps_up[b][:, :], hid_scale[:, :], sgate, ALU.mult,
                                               ALU.mult).then_inc(hid_ready, 1)

            def hidden_low(t):
                dve.wait_ge(hT_high_ready, t + 1)
                nc.vector.scalar_tensor_tensor(hT_low, hT_high, -LOW_SHIFT,
                                               ps_hidT[:, :].rearrange("p (c t) -> p c t", c=HC), ALU.mult,
                                               ALU.add).then_inc(hT_low_ready, 1)

            def row_weights(t, u):
                dve.wait_ge(rows_loaded[u], 4 * (t - u) + 16)
                if not (isinstance(t, int) and t < RING):
                    dve.wait_ge(added, 16 * (t - RING + 1))
                e_t = expert_f[:, t:t + 1] if isinstance(t, int) else expert_f[:, bass.ds(t, 1)]
                nc.vector.tensor_tensor(is_first[:, :], xr[:, u, FIRST_EXPERT:FIRST_EXPERT + 1], e_t,
                                        ALU.is_equal).then_inc(w_step, 1)
                nc.vector.tensor_copy(token_of[:, u, :], xr[:, u, TOKEN:TOKEN + 1].bitcast(U32)).then_inc(w_step, 1)
                dve.wait_ge(w_step, 3 * t + 2)
                nc.vector.scalar_tensor_tensor(w_row[:, u % 2, :], is_first[:, :], xr[:, u, W_GAP:W_GAP + 1],
                                               xr[:, u, W_SECOND:W_SECOND + 1], ALU.mult, ALU.add).then_inc(w_step, 1)

            def weigh(t, u):
                b = u % 2
                dve.wait_ge(w_step, 3 * t + 3)
                dve.wait_ge(down_psum, t + 1)
                nc.vector.tensor_scalar(y[:, u, :], ps_down[b][:, 0:dim], w_row[:, b, :], y_unscale[:, :],
                                        ALU.mult, ALU.mult).then_inc(y_ready, 1)

            def step2(t, u):
                if alive2(t + 1):
                    rows_low(t + 1, (u + 1) % RING)
                if alive2(t - 1):
                    hidden_low(t - 1)
                if alive2(t):
                    row_weights(t, u)
                if alive2(t):
                    hidden_product(t, u)
                if alive2(t - 1):
                    weigh(t - 1, (u + 3) % RING)

            over_routed(dve, step2)

        @block.gpsimd
        def _(pool):
            nc.gpsimd.memset(state[:, :, :, :], 0.0).then_inc(init_done, 1)
            nc.gpsimd.memset(kacc[:, :, :], 0.0).then_inc(init_done, 1)
            nc.gpsimd.memset(macc[:, :], 0.0).then_inc(init_done, 1)
            pool.wait_ge(init_done, 4)
            pool.wait_ge(consts_in, 16)
            pool.wait_ge(table_step, 1)
            pool.dma_start(out[tokens:tokens + P, :], pad_rows[:, 0:dim]).then_inc(spare_zeroed, 16)

            def rstd_first(n, u):
                b = u % 2
                pool.wait_ge(var1_ready, n + 1)
                if later(n, 2):
                    pool.wait_ge(xhat_ready, n - 1)
                nc.gpsimd.tensor_tensor(rstd1[:, b, :], var1[:, b, :], minus_half, ALU.pow).then_inc(rstd1_ready, 1)

            def rotated(n, u):
                pool.wait_ge(rot_parts_ready, 3 * n + 3)
                if later(n):
                    pool.wait_ge(exp_ready, 2 * n)
                nc.gpsimd.tensor_tensor(rot[:, :], rot_a[:, :], rot_b[:, :], ALU.add).then_inc(rot_ready, 1)

            def mask(n, u):
                pool.wait_ge(attn_copied, n + 1)
                nc.gpsimd.tensor_tensor(attn[:, 1, :, :], attn[:, 1, :, :],
                                        causal.unsqueeze(1).to_broadcast([P, 4, P]), ALU.mult).then_inc(attn_pool, 1)

            def state_sum(n, u):
                b = u % 2
                pool.wait_ge(state_add_ready, n + 1)
                pool.wait_ge(num_psum, n + 1)
                if later(n, 2):
                    pool.wait_ge(state_ready, n - 1)
                nc.gpsimd.tensor_tensor(state[:, b, :, :], state[:, b, :, :], state_add[:, :, :],
                                        ALU.add).then_inc(state_ready, 1)

            def key_sum(n, u):
                b = u % 2
                pool.wait_ge(kcum_psum, n + 1)
                pool.wait_ge(phi_ready, n + 1)
                if later(n, 2):
                    pool.wait_ge(kacc_ready, n - 1)
                nc.gpsimd.tensor_tensor(kacc[:, b, :], kacc[:, b, :], phi[:, b, dim:2 * dim],
                                        ALU.add).then_inc(kacc_ready, 1)

            def scale_q(n, u):
                b = u % 2
                pool.wait_ge(rden_ready, n + 1)
                if later(n):
                    pool.wait_ge(qT_psum, n)
                nc.gpsimd.tensor_tensor(qn[:, :].rearrange("p (h d) -> p h d", d=HEAD_DIM),
                                        phi[:, b, 0:dim].rearrange("p (h d) -> p h d", d=HEAD_DIM),
                                        rden[:, :].unsqueeze(2).to_broadcast([P, heads, HEAD_DIM]),
                                        ALU.mult).then_inc(qn_ready, 1)

            def roots_second(n):
                pool.wait_ge(var2_ready, 2 * n + 2)
                if later(n):
                    pool.wait_ge(rms2_ready, n)
                nc.gpsimd.tensor_tensor(inv2[:, :], var2[:, :], minus_half.to_broadcast([P, 2]),
                                        ALU.pow).then_inc(inv2_ready, 1)

            def accumulate(n, u):
                pool.wait_ge(xhat2_ready, n + 1)
                if not first_round(n):
                    pool.wait_ge(acc_stored[u], 4 * (n - u))
                nc.gpsimd.tensor_tensor(acc[:, u, :], x1[:, :], xhat2[:, :], ALU.add).then_inc(acc_ready, 1)

            def token_column(n, u):
                if not first_round(n):
                    pool.wait_ge(scattered[u], 8 * (n - u))
                nc.gpsimd.tensor_copy(rows[:, u, TOKEN:TOKEN + 1].bitcast(U32),
                                      ids[:, n:n + 1] if isinstance(n, int) else ids[:, bass.ds(n, 1)]).then_inc(tok_ready, 1)

            def member_sum(n, u):
                b = u % 2
                pool.wait_ge(ranks_psum, n + 1)
                pool.wait_ge(members_ready, n + 1)
                if later(n):
                    pool.wait_ge(macc_ready, n)
                nc.gpsimd.tensor_tensor(macc[:, :], macc[:, :], members[:, b, :], ALU.add).then_inc(macc_ready, 1)

            def scatter(n, u):
                b = u % 2
                pool.wait_ge(slots_ready, n + 1)
                pool.wait_ge(meta_ready, 3 * n + 3)
                pool.wait_ge(xn_ready, n + 1)
                pool.wait_ge(tok_ready, n + 1)
                settle(pool)
                for k in range(2):
                    pool.indirect_dma_start(out=routed_rows[:, :],
                                            out_offset=bass.IndirectOffsetOnAxis(ap=slot_of[:, u, k:k + 1], axis=0),
                                            in_=rows[:, u, :], in_offset=None).then_inc(scattered[u], 16)

            def step(n, u):
                m, um, ua, ur = n + 1, (u + 1) % RING, (u + 3) % RING, (u + 1) % RING
                behind = isinstance(n, int) and n >= tiles
                if isinstance(n, int) and n == 0:
                    pool.wait_ge(weights_in, 16 * 6)
                if isinstance(n, int) and n == experts + 2:
                    pool.wait_ge(norms_ready, 2)
                    nc.gpsimd.tensor_tensor(inv_norms[:, :], norms2[:, :], minus_half.to_broadcast([P, 3]),
                                            ALU.pow).then_inc(inv_norms_ready, 1)
                if alive(n + 2):
                    rstd_first(n + 2, (u + 2) % RING)
                if alive(m):
                    rotated(m, um)
                if alive(n - 4) and not behind:
                    scatter(n - 4, u)
                if alive(n):
                    mask(n, u)
                if alive(n - 3) and behind:
                    member_sum(n - 3, ur)
                if alive(n - 1):
                    roots_second(n - 1)
                    token_column(n - 1, ua)
                    accumulate(n - 1, ua)
                if alive(n):
                    state_sum(n, u)
                if alive(m):
                    scale_q(m, um)
                    key_sum(m, um)
                if alive(n - 3) and not behind:
                    member_sum(n - 3, ur)
                if alive(n - 4) and behind:
                    scatter(n - 4, u)

            over_tiles(pool, step)

            for u in range(RING):
                pool.wait_ge(acc_stored[u], 16 * (tiles // RING))
            pool.wait_ge(spare_zeroed, 16)

            def step2(t, u):
                if not alive2(t - 1):
                    return
                t, u = t - 1, (u + 3) % RING
                pool.wait_ge(y_ready, t + 1)
                if not (isinstance(t, int) and t < 1):
                    pool.wait_ge(added, 16 * t)
                settle(pool)
                pool.indirect_dma_start(
                    out=out[:, :], out_offset=bass.IndirectOffsetOnAxis(ap=token_of[:, u, :], axis=0),
                    in_=y[:, u, :], in_offset=None, compute_op=ALU.add).then_inc(added, 16)

            over_routed(pool, step2)
            pool.wait_ge(added, 16 * routed_tiles)

        @block.tensor
        def _(pe):
            pe.wait_ge(consts_in, 16)
            pe.wait_ge(init_done, 4)

            def transposes(dst, src, chunks):
                for c in range(chunks):
                    last = nc.tensor.transpose(dst[:, c * P:(c + 1) * P], src[:, c * P:(c + 1) * P], ident)
                return last

            def product(dst, lhs, rhs, chunks):
                for c in range(chunks):
                    last = nc.tensor.matmul(dst, lhs(c), rhs(c), start=c == 0, stop=c == chunks - 1)
                return last

            def transpose_x(n, u):
                pe.wait_ge(xhat_ready, n + 1)
                if later(n, 2):
                    pe.wait_ge(qT_ready, n - 1)
                transposes(ps_qT[:, dim:2 * dim], xhat[:, u % 2, :], KC).then_inc(xhatT_psum, 1)

            def scores(n, u):
                pe.wait_ge(kT_ready, n + 1)
                if later(n):
                    pe.wait_ge(yT_ready, n)
                    pe.wait_ge(state_add_ready, n)
                for i in range(2):
                    pe.wait_ge(q_head_ready, 8 * n + 4 * i + 4)
                    for c in range(KC):
                        nc.tensor.matmul(ps_scores[2 * i + c][:, :], kT[:, c, :], q_head[:, 4 * i:4 * i + 4, c, :],
                                         start=True, stop=True).then_inc(scores_psum, 1)

            def project_qk(n, u):
                b = u % 2
                pe.wait_ge(xhatT_ready, n + 1)
                if later(n):
                    pe.wait_ge(rot_parts_ready, 3 * n)
                product(ps_qk[:, :], lambda c: xhatT[:, b, c, :], lambda c: wqk_sb[:, c, :], KC).then_inc(qk_psum, 1)

            def project_v(n, u):
                b = u % 2
                if later(n):
                    pe.wait_ge(kT_ready, n)
                product(ps_xv[:, dim:2 * dim], lambda c: xhatT[:, b, c, :], lambda c: wv_sb[:, c, :], KC).then_inc(v_psum, 1)

            def v_of(b, c):
                v = v_pad[:, b, 8 * c:8 * c + 8, :].rearrange("p (a b) (c d) -> p a (b c) d", b=2, c=2)
                return v[:, :, 0:4:3, :]

            def state_product(n, u):
                b = u % 2
                pe.wait_ge(attn_copied, n + 1)
                pe.wait_ge(v_ready, n + 1)
                for c in range(KC):
                    last = nc.tensor.matmul(ps_state[:, c * P:(c + 1) * P], phi[:, b, dim + c * P:dim + (c + 1) * P],
                                            v_of(b, c), start=True, stop=True)
                last.then_inc(state_psum, 1)

            def attend(n, u):
                b = u % 2
                pe.wait_ge(attn_dve, 3 * n + 2)
                pe.wait_ge(qT_ready, n + 1)
                if later(n, 2):
                    pe.wait_ge(state_ready, n - 1)
                for c in range(KC):
                    nc.tensor.matmul(ps_num[:, c * P:(c + 1) * P], state[:, b, c, :], qT[:, c, :],
                                     start=c == 0, stop=False, skip_group_check=True)
                for c in range(KC):
                    if c == 1:
                        pe.wait_ge(attn_dve, 3 * n + 3)
                        pe.wait_ge(attn_pool, n + 1)
                    for par in range(2):
                        for g in range(4):
                            last = nc.tensor.matmul(ps_num[32 * g:32 * g + 32, c * P:(c + 1) * P],
                                                    v_pad[:, b, 8 * c + 2 * g + par, :],
                                                    attn[:, 2 * (g // 2) + c, 2 * (g % 2) + par, :],
                                                    start=False, stop=c == KC - 1 and par == 1, skip_group_check=True)
                last.then_inc(num_psum, 1)

            def key_prefix(n, u):
                b = u % 2
                pe.wait_ge(phi_ready, n + 1)
                if later(n, 2):
                    pe.wait_ge(kacc_ready, n - 1)
                if later(n, 4):
                    pe.wait_ge(rank_step, 2 * (n - 4) + 1)
                elif later(n, 2):
                    pe.wait_ge(x1_ready, n - 1)
                k = phi[:, b, dim:2 * dim]
                nc.tensor.matmul(ps_small[:, 0:dim], causal, k, start=True, stop=False)
                nc.tensor.matmul(ps_small[:, 0:dim], ones, kacc[:, b, :], start=False, stop=True).then_inc(kcum_psum, 1)
                if later(n, 3):
                    pe.wait_ge(xnT_ready, n - 2)
                transposes(ps_xv[:, dim:2 * dim], k, KC).then_inc(kT_psum, 1)

            def output_projection(n, u):
                pe.wait_ge(yT_ready, n + 1)
                if later(n, 2):
                    pe.wait_ge(route_step, 5 * (n - 2) + 1)
                product(ps_small[:, 0:dim], lambda c: yT[:, c, :], lambda c: wo_sb[:, c, :], KC).then_inc(wo_psum, 1)

            def transpose_xn(n, u):
                pe.wait_ge(xn_ready, n + 1)
                if n + 3 < tiles if isinstance(n, int) else True:
                    pe.wait_ge(v_ready, n + 4)
                transposes(ps_xv, rows[:, u, 0:dim], KC).then_inc(xnT_psum, 1)

            def logits(n, u):
                pe.wait_ge(xnT_ready, n + 1)
                product(ps_small[:, 256:256 + experts], lambda c: xnT[:, c, :], lambda c: wr_sb[:, c, :], KC).then_inc(logits_psum, 1)

            def ranks(n, u):
                pe.wait_ge(members_ready, n + 1)
                if later(n):
                    pe.wait_ge(macc_ready, n)
                if n + 2 < tiles if isinstance(n, int) else True:
                    pe.wait_ge(x1_ready, n + 3)
                else:
                    pe.wait_ge(route_step, 5 * n + 1)
                if isinstance(n, int) and n == experts - 2:
                    pe.wait_ge(square_sum_ready, 1)
                    nc.tensor.matmul(ps_small[:, 280:282], ones, square_sum[:, :], start=True,
                                     stop=True).then_inc(norms_psum, 1)
                nc.tensor.matmul(ps_small[:, 264:264 + experts], earlier, members[:, u % 2, :], start=True, stop=False)
                nc.tensor.matmul(ps_small[:, 264:264 + experts], ones_b, macc[:, :], start=False, stop=True).then_inc(ranks_psum, 1)

            def transpose_q(n, u):
                pe.wait_ge(qn_ready, n + 1)
                if later(n):
                    pe.wait_ge(qT_ready, n)
                transposes(ps_qT, qn[:, :], KC).then_inc(qT_psum, 1)

            def step(n, u):
                m, um, ua, uc, ur = n + 1, (u + 1) % RING, (u + 3) % RING, (u + 2) % RING, (u + 1) % RING
                if isinstance(n, int) and n == -1:
                    pe.wait_ge(qkv_in, 16 * 2)
                if isinstance(n, int) and n == 0:
                    pe.wait_ge(weights_in, 16 * 6)
                if alive(m):
                    project_qk(m, um)
                if alive(n - 3):
                    if alive(n):
                        pe.wait_ge(kcum_read, n + 1)
                    else:
                        pe.wait_ge(rank_step, 2 * (n - 4) + 1)
                    logits(n - 3, ur)
                if alive(n):
                    transpose_q(n, u)
                if alive(m):
                    project_v(m, um)
                if alive(n - 1):
                    output_projection(n - 1, ua)
                if alive(n):
                    scores(n, u)
                if alive(n):
                    state_product(n, u)
                if alive(n - 2):
                    transpose_xn(n - 2, uc)
                if alive(n - 3):
                    ranks(n - 3, ur)
                if alive(n + 2):
                    transpose_x(n + 2, (u + 2) % RING)
                if alive(n):
                    attend(n, u)
                if alive(m):
                    key_prefix(m, um)

            over_tiles(pe, step)

            pe.wait_ge(macc_ready, tiles)
            pe.wait_ge(rank_step, 2 * tiles - 1)
            pe.wait_ge(route_step, 5 * tiles - 4)
            nc.tensor.matmul(ps_small[:, 272:272 + experts], ones_b, macc[:, :], start=True, stop=True).then_inc(counts_psum, 1)

            pe.wait_ge(low_ready, up_pieces + 2)
            pe.wait_ge(table_ready, 2)

            def transpose_rows(t, u):
                pe.wait_ge(rows_loaded[u], 4 * (t - u) + 16)
                if not (isinstance(t, int) and t < 1):
                    pe.wait_ge(xT_low_ready, t)
                transposes(ps_xrT, xr[:, u, 0:dim], KC).then_inc(xrT_psum, 1)

            def expert_of(t):
                return pe.value_load(expert_u[0:1, t:t + 1] if isinstance(t, int) else expert_u[0:1, bass.ds(t, 1)],
                                     min_val=0, max_val=experts - 1)

            def up(t, u, e):
                b = u % 2
                pe.wait_ge(xT_low_ready, t + 1)
                if not (isinstance(t, int) and t < 2):
                    pe.wait_ge(sgate_ready, t - 1)
                    pe.wait_ge(hid_ready, t - 1)
                for half, dst, signal in [(1, ps_gate, gate_psum), (0, ps_up, up_psum)]:
                    products = [(xT_high, c, part) for c in range(KC) for part in range(2)]
                    products += [(xT_low, c, 0) for c in range(KC)]
                    for k, (rows_T, c, part) in enumerate(products):
                        j = c * 2 + half
                        w = up_of[:, bass.ds(e, 1), j * PIECE:(j + 1) * PIECE].rearrange("p e n -> p (e n)").bitcast(F16)
                        last = nc.tensor.matmul(dst[b][:, :], rows_T[:, b, c, :], w[:, part * PIECE:(part + 1) * PIECE],
                                                start=k == 0, stop=k == len(products) - 1)
                    last.then_inc(signal, 1)

            def transpose_hidden(t, u):
                pe.wait_ge(hid_ready, t + 1)
                if not (isinstance(t, int) and t < 1):
                    pe.wait_ge(hT_low_ready, t)
                transposes(ps_hidT, hid[:, u % 2, :], HC).then_inc(hidT_psum, 1)

            def down(t, u):
                b = u % 2
                e = expert_of(t)
                pe.wait_ge(hT_low_ready, t + 1)
                if isinstance(t, int) and t == 0:
                    pe.wait_ge(down_low_ready, down_pieces + 2)
                    pe.wait_ge(down_small_ready, down_pieces)
                if not (isinstance(t, int) and t < 2):
                    pe.wait_ge(y_ready, t - 1)
                high_low = down_of[:, bass.ds(e, 1), :].rearrange("p e n -> p (e n)")
                small = down_small_of[:, bass.ds(e, 1), :].rearrange("p e n -> p (e n)")
                for c in range(HC):
                    j, at0 = c * dim // PIECE, c * dim % PIECE
                    parts = high_low[:, j * PIECE:(j + 1) * PIECE].bitcast(F16)
                    for k, (hidden_T, w) in enumerate([(hT_high, parts[:, at0:at0 + dim]),
                                                       (hT_high, parts[:, PIECE + at0:PIECE + at0 + dim]),
                                                       (hT_low, small[:, c * dim:(c + 1) * dim])]):
                        last = nc.tensor.matmul(ps_down[b][:, 0:dim], hidden_T[:, c, :], w,
                                                start=c == 0 and k == 0, stop=c == HC - 1 and k == 2)
                last.then_inc(down_psum, 1)

            def step2(t, u):
                e = expert_of(t) if alive2(t) else None
                if alive2(t + 1):
                    transpose_rows(t + 1, (u + 1) % RING)
                if alive2(t - 1):
                    transpose_hidden(t - 1, (u + 3) % RING)
                if alive2(t):
                    up(t, u, e)
                if alive2(t - 1):
                    down(t - 1, (u + 3) % RING)

            over_routed(pe, step2)


_B, _T, _D, _E, _H = 2, 2048, 256, 8, 512


def kernel(**inputs):
    import numpy as np
    import concourse.bacc as bacc
    from concourse.bass_utils import run_bass_kernel_spmd

    f32 = np.float32
    tokens, tiles, region, routed = sizes(_B, _T, _D, _E, _H)

    def arr(name):
        return np.asarray(inputs[name])

    half = HEAD_DIM // 2
    inv_freq = f32(10000.0) ** (-np.arange(half, dtype=f32) / f32(half))
    angle = np.arange(_T, dtype=f32)[:, None] * inv_freq.astype(f32)[None, :]
    cos, sin = np.cos(angle), np.sin(angle)
    s, t = np.arange(P)[:, None], np.arange(P)[None, :]
    rep = lambda row: np.broadcast_to(np.asarray(row, f32).reshape(1, -1), (P, np.asarray(row).size))
    head = np.arange(P)[:, None] // HEAD_DIM == np.arange(P // HEAD_DIM)[None, :]
    consts_f = np.concatenate([
        s == t, s <= t, np.ones((P, P)), s // HEAD_DIM == t // HEAD_DIM, head,
        rep(np.arange(_E)), rep(np.arange(32) * P), rep(np.tril(np.ones((_E, _E)))),
        rep(np.arange(routed)), rep(np.arange(_E) * region), rep([-0.5])], axis=1).astype(f32)
    import ml_dtypes
    consts_b = np.concatenate([s < t, np.ones((P, P))], axis=1).astype(ml_dtypes.bfloat16)
    n = np.arange(tiles)
    token_ids = ((n % 2) * _T + (n // 2) * P)[None, :] + np.arange(P)[:, None]
    token_ids = np.concatenate([token_ids, tokens + np.arange(P)[:, None]], axis=1).astype(np.uint32)

    def chunked(w):
        e, o, i = w.shape
        return np.ascontiguousarray(w.transpose(2, 0, 1).reshape(i // P, P, e, o).transpose(1, 2, 0, 3).reshape(P, e, -1))

    arrays = {
        "x": arr("L0_attn_x").reshape(tokens, _D),
        "w_qk": np.ascontiguousarray(np.concatenate([arr("L0_attn_Wq").T, arr("L0_attn_Wk").T], axis=1)),
        "w_v": np.ascontiguousarray(arr("L0_attn_Wv").T),
        "w_o": np.ascontiguousarray(arr("L0_attn_Wo").T),
        "rope": np.ascontiguousarray(np.concatenate([cos, cos, -sin, sin], axis=1).astype(f32)
                                     .reshape(_T // P, P, 2 * HEAD_DIM).transpose(1, 0, 2).reshape(P, -1)),
        "norm_scale": arr("L0_ffn_norm_scale").reshape(1, _D),
        "w_router": np.ascontiguousarray(arr("L0_ffn_w_router").T),
        "w_up": chunked(arr("L0_ffn_w_up")),
        "w_down": chunked(arr("L0_ffn_w_down")),
        "consts_f": consts_f,
        "consts_b": consts_b,
        "token_ids": token_ids,
    }
    nc = bacc.Bacc("TRN2", target_bir_lowering=False, num_devices=1)
    aps = [nc.dram_tensor(k, a.shape, mybir.dt.from_np(a.dtype), kind="ExternalInput").ap() for k, a in arrays.items()]
    routed_rows = nc.dram_tensor("routed_rows", [_E * region + P, ROW], F32, kind="Internal").ap()
    out = nc.dram_tensor("out", [tokens + P, _D], F32, kind="ExternalOutput").ap()
    block_kernel(nc, *aps, routed_rows, out, _B, _T, _E, _H)
    r = run_bass_kernel_spmd(nc, [arrays], core_ids=[0])
    return np.asarray(r.results[0]["out"])[0:tokens].reshape(_B, _T, _D)
```
